# Optimizing a Trainium2 kernel written in Bass

```python
import numpy as np
import jax
import jax.numpy as jnp

def _softmax(x, axis=-1):
    return jax.nn.softmax(x, axis=axis)

def _gelu(x):
    return jax.nn.gelu(x, approximate=True)

def _silu(x):
    return jax.nn.silu(x)

def _sigmoid(x):
    return jax.nn.sigmoid(x)

def _layernorm(x, axis=-1, eps=1e-05):
    m = jnp.mean(x, axis=axis, keepdims=True)
    v = jnp.var(x, axis=axis, keepdims=True)
    return (x - m) / jnp.sqrt(v + eps)

def _scatter_add(tgt, idx, src, axis=0):
    return tgt.at[idx].add(src)

def _segment_sum(src, seg, n):
    return jax.ops.segment_sum(src, seg, n)
kernel_name = 'mk_seq_postln_d1_jaxref_r8_6acab3'

def setup_inputs(seed: int=0):
    np.random.seed(seed)
    _w = jnp.asarray

    def _L0_attn_setup():
        import jax, jax.numpy as jnp
        import numpy as np
        import math
        D_MODEL = 128
        EMB = 128
        key = jax.random.key(seed)
        ks = jax.random.split(key, 9)
        s = 1.0 / math.sqrt(EMB)
        x = jax.random.normal(ks[0], (4, 256, EMB), dtype=jnp.float32)
        W1 = jax.random.uniform(ks[1], (EMB, EMB), minval=-s, maxval=s)
        b1 = jax.random.uniform(ks[2], (EMB,), minval=-s, maxval=s)
        W2 = jax.random.uniform(ks[3], (EMB, EMB), minval=-s, maxval=s)
        b2 = jax.random.uniform(ks[4], (EMB,), minval=-s, maxval=s)
        W3 = jax.random.uniform(ks[5], (EMB, EMB), minval=-s, maxval=s)
        b3 = jax.random.uniform(ks[6], (EMB,), minval=-s, maxval=s)
        W4 = jax.random.uniform(ks[7], (EMB, EMB), minval=-s, maxval=s)
        b4 = jax.random.uniform(ks[8], (EMB,), minval=-s, maxval=s)
        return {'x': x, 'W1': W1, 'b1': b1, 'W2': W2, 'b2': b2, 'W3': W3, 'b3': b3, 'W4': W4, 'b4': b4}
    _L0_attn_in = _L0_attn_setup()

    def _L0_ffn_setup():
        import jax, jax.numpy as jnp
        import numpy as np
        B, S, H = (2, 256, 128)
        E, F, K = (64, 64, 8)
        G, TG = (8, 4)
        SCALE = 2.5
        F_SH = 64

        def _gate(x, gate_w, gate_bias):
            scores = jax.nn.sigmoid(x @ gate_w.T)
            sc = scores + gate_bias[None, :]
            T = x.shape[0]
            group_scores = jax.lax.top_k(sc.reshape(T, G, E // G), 2)[0].sum(-1)
            _, gidx = jax.lax.top_k(group_scores, TG)
            gmask = jnp.zeros((T, G), sc.dtype).at[jnp.arange(T)[:, None], gidx].set(1.0)
            smask = jnp.repeat(gmask, E // G, axis=1)
            masked = jnp.where(smask > 0, sc, -jnp.inf)
            _, tidx = jax.lax.top_k(masked, K)
            tw = jnp.take_along_axis(scores, tidx, axis=1)
            tw = tw / (tw.sum(-1, keepdims=True) + 1e-20)
            return (tidx, tw * SCALE)
        key = jax.random.key(seed)
        ks = jax.random.split(key, 9)

        def w(k, shape, fan_in):
            return jax.random.normal(k, shape, jnp.float32) / np.float32(np.sqrt(fan_in))
        return {'hidden_states': jax.random.normal(ks[0], (B, S, H), jnp.float32), 'gate_w': w(ks[1], (E, H), H), 'gate_bias': jax.random.normal(ks[2], (E,), jnp.float32) * 0.01, 'We_gate': w(ks[3], (E, H, F), H), 'We_up': w(ks[4], (E, H, F), H), 'We_down': w(ks[5], (E, F, H), F), 'Ws_gate': w(ks[6], (H, F_SH), H), 'Ws_up': w(ks[7], (H, F_SH), H), 'Ws_down': w(ks[8], (F_SH, H), F_SH)}
    _L0_ffn_in = _L0_ffn_setup()
    _d = {'L0_attn_x': _L0_attn_in['x'], 'L0_attn_W1': _L0_attn_in['W1'], 'L0_attn_b1': _L0_attn_in['b1'], 'L0_attn_W2': _L0_attn_in['W2'], 'L0_attn_b2': _L0_attn_in['b2'], 'L0_attn_W3': _L0_attn_in['W3'], 'L0_attn_b3': _L0_attn_in['b3'], 'L0_attn_W4': _L0_attn_in['W4'], 'L0_attn_b4': _L0_attn_in['b4'], 'L0_ffn_gate_w': _L0_ffn_in['gate_w'], 'L0_ffn_gate_bias': _L0_ffn_in['gate_bias'], 'L0_ffn_We_gate': _L0_ffn_in['We_gate'], 'L0_ffn_We_up': _L0_ffn_in['We_up'], 'L0_ffn_We_down': _L0_ffn_in['We_down'], 'L0_ffn_Ws_gate': _L0_ffn_in['Ws_gate'], 'L0_ffn_Ws_up': _L0_ffn_in['Ws_up'], 'L0_ffn_Ws_down': _L0_ffn_in['Ws_down']}
    _x0 = _d['L0_attn_x']
    _d['L0_attn_x'] = jax.random.normal(jax.random.fold_in(jax.random.key(seed), 1), (4, 1024, 128), dtype=_x0.dtype)
    del _x0
    return _d

def reference(L0_attn_x, L0_attn_W1, L0_attn_b1, L0_attn_W2, L0_attn_b2, L0_attn_W3, L0_attn_b3, L0_attn_W4, L0_attn_b4, L0_ffn_gate_w, L0_ffn_gate_bias, L0_ffn_We_gate, L0_ffn_We_up, L0_ffn_We_down, L0_ffn_Ws_gate, L0_ffn_Ws_up, L0_ffn_Ws_down):

    def _L0_attn_ref(x, W1, b1, W2, b2, W3, b3, W4, b4):
        import jax, jax.numpy as jnp
        import numpy as np
        import math
        D_MODEL = 128
        EMB = 128
        Q = x @ W1 + b1
        K = x @ W2 + b2
        V = x @ W3 + b3
        scale = 1.0 / math.sqrt(D_MODEL)
        scores = jnp.einsum('bse,bte->bst', Q, K) * scale
        attn = jax.nn.softmax(scores, axis=-1)
        out = jnp.einsum('bst,bte->bse', attn, V)
        return out @ W4 + b4

    def _L0_ffn_ref(hidden_states, gate_w, gate_bias, We_gate, We_up, We_down, Ws_gate, Ws_up, Ws_down):
        import jax, jax.numpy as jnp
        import numpy as np
        B, S, H = (2, 256, 128)
        E, F, K = (64, 64, 8)
        G, TG = (8, 4)
        SCALE = 2.5
        F_SH = 64

        def _gate(x, gate_w, gate_bias):
            scores = jax.nn.sigmoid(x @ gate_w.T)
            sc = scores + gate_bias[None, :]
            T = x.shape[0]
            group_scores = jax.lax.top_k(sc.reshape(T, G, E // G), 2)[0].sum(-1)
            _, gidx = jax.lax.top_k(group_scores, TG)
            gmask = jnp.zeros((T, G), sc.dtype).at[jnp.arange(T)[:, None], gidx].set(1.0)
            smask = jnp.repeat(gmask, E // G, axis=1)
            masked = jnp.where(smask > 0, sc, -jnp.inf)
            _, tidx = jax.lax.top_k(masked, K)
            tw = jnp.take_along_axis(scores, tidx, axis=1)
            tw = tw / (tw.sum(-1, keepdims=True) + 1e-20)
            return (tidx, tw * SCALE)
        b, s, h = hidden_states.shape
        x = hidden_states.reshape(-1, h).astype(jnp.float32)
        tidx, tw = _gate(x, gate_w, gate_bias)
        T = x.shape[0]
        w_dense = jnp.zeros((T, E), tw.dtype).at[jnp.arange(T)[:, None], tidx].add(tw)

        def body(acc, ws):
            wg, wu, wdn, cw = ws
            hmid = jax.nn.silu(x @ wg) * (x @ wu)
            return (acc + cw[:, None] * (hmid @ wdn), None)
        y, _ = jax.lax.scan(body, jnp.zeros_like(x), (We_gate, We_up, We_down, w_dense.T))
        y = y.reshape(b, s, h)
        shared = jax.nn.silu(hidden_states @ Ws_gate) * (hidden_states @ Ws_up) @ Ws_down
        return y + shared
    x = L0_attn_x
    x = _layernorm(x + _L0_attn_ref(x, L0_attn_W1, L0_attn_b1, L0_attn_W2, L0_attn_b2, L0_attn_W3, L0_attn_b3, L0_attn_W4, L0_attn_b4), axis=-1)
    x = _layernorm(x + _L0_ffn_ref(x, L0_ffn_gate_w, L0_ffn_gate_bias, L0_ffn_We_gate, L0_ffn_We_up, L0_ffn_We_down, L0_ffn_Ws_gate, L0_ffn_Ws_up, L0_ffn_Ws_down), axis=-1)
    return x

_drawn_inputs = setup_inputs


def setup_inputs(seed=0):
    import zlib

    import numpy as np

    out = dict(_drawn_inputs(seed))
    spreads = {}
    factors = {'L0_attn_b1': 4.085, 'L0_attn_b2': 8.0}
    for name, (base, spread) in spreads.items():
        noise = np.random.default_rng([zlib.crc32(name.encode()), seed]).standard_normal(out[name].shape)
        drawn = base * np.exp(spread * noise) if base else spread * noise
        out[name] = jnp.asarray(drawn.astype(out[name].dtype))
    for name, factor in factors.items():
        out[name] = (out[name] * factor).astype(out[name].dtype)
    return out
```

```python
from contextlib import ExitStack

import concourse.bass as bass
from concourse import mybir

F32 = mybir.dt.float32
F32R = mybir.dt.float32r
ALU = mybir.AluOpType
ACT = mybir.ActivationFunctionType
AX = mybir.AxisListType

P = 128
HALF = 512
EPS = 1e-5
ROUTE_SCALE = 2.5
TOP_GROUPS = 4
FAR = 1e30
GONE = -3e38
UNROLL = 4


def block_kernel(nc, x, w_qkvo, b_qkvo, gate_wT, gate_bias, w_pairs, ident_in, lower_in, w_scratch, out):
    B, S, D = x.shape
    E = gate_wT.shape[1]
    F = P // 2
    GROUPS = 8
    NT = S // P
    NH = S // HALF
    TPH = HALF // P
    PAIRS = E // 2
    QP = PAIRS + 1
    STEPS = QP * NH
    SCALE = float(D) ** -0.5
    assert D == P and NH == 2 and E == 64 and w_pairs.shape[0] == QP and PAIRS % UNROLL == 0

    ctx = ExitStack()
    with ctx:
        def sb(name, shape, dt=F32):
            return ctx.enter_context(nc.sbuf_tensor(name, shape, dt))

        ident = sb("ident", [P, P])
        identr = sb("identr", [P, P], F32R)
        lower = sb("lower", [P, GROUPS, GROUPS])
        wq, wk, wv, wo = (sb(n, [P, P]) for n in ("wq", "wk", "wv", "wo"))
        wq_s = sb("wq_s", [P, P])
        bq_s = sb("bq_s", [P, 1])
        bias_cols = sb("bias_cols", [P, 4])
        bo_row = sb("bo_row", [P, P])
        bv_spread = sb("bv_spread", [P, P])
        b_row = sb("b_row", [P, P])
        gwT = sb("gwT", [P, E])
        gbias = sb("gbias", [P, E])
        minus_half = sb("minus_half", [P, TPH])
        x_tok = sb("x_tok", [P, NT, D])
        xT = sb("xT", [P, S])
        qT_hi, qT_lo, kT_hi, kT_lo = (sb(n, [P, S], F32R) for n in ("qT_hi", "qT_lo", "kT_hi", "kT_lo"))
        v_hi = sb("v_hi", [P, NT, D], F32R)
        v_lo = sb("v_lo", [P, NT, D], F32R)
        neg_max = sb("neg_max", [P, NT])
        row_sum = sb("row_sum", [P, NT])
        inv_sum = sb("inv_sum", [P, NT])
        probs = sb("probs", [P, 2, S])
        pT_hi = sb("pT_hi", [P, NT, HALF], F32R)
        pT_lo = sb("pT_lo", [P, NT, HALF], F32R)
        oT = sb("oT", [P, HALF])
        x_b = sb("x_b", [P, NT, D])
        x_res = sb("x_res", [P, NT, D])
        x1 = sb("x1", [P, NT, D])
        bn = sb("bn", [P, NT, 6])
        mv = sb("mv", [P, NT, 2])
        var_eps = sb("var_eps", [P, NT])
        rstd = sb("rstd", [P, NT])
        x1T = sb("x1T", [P, S])
        x1T_hi = sb("x1T_hi", [P, S], F32R)
        x1T_lo = sb("x1T_lo", [P, S], F32R)
        exp_neg = sb("exp_neg", [P, NT, E])
        denom = sb("denom", [P, E])
        sig = sb("sig", [P, E])
        biased = sb("biased", [P, GROUPS, E // GROUPS])
        hi4, lo4 = sb("hi4", [P, GROUPS, 4]), sb("lo4", [P, GROUPS, 4])
        hi2, lo2, mn2, mx2 = (sb(n, [P, GROUPS, 2]) for n in ("hi2", "lo2", "mn2", "mx2"))
        hi1, lo1, mn1, mx1 = (sb(n, [P, GROUPS, 1]) for n in ("hi1", "lo1", "mn1", "mx1"))
        g_score = sb("g_score", [P, GROUPS])
        beats = sb("beats", [P, GROUPS, GROUPS])
        ties = sb("ties", [P, GROUPS, GROUPS])
        ties_low = sb("ties_low", [P, GROUPS, GROUPS])
        beaten = sb("beaten", [P, GROUPS, GROUPS])
        rank = sb("rank", [P, GROUPS])
        g_in = sb("g_in", [P, GROUPS])
        g_out = sb("g_out", [P, GROUPS])
        kept = sb("kept", [P, GROUPS, E // GROUPS])
        masked = sb("masked", [P, GROUPS, E // GROUPS])
        top8 = sb("top8", [P, 8])
        replaced = sb("replaced", [P, E])
        chosen = sb("chosen", [P, E])
        w_raw8 = sb("w_raw8", [P, E])
        w_sum = sb("w_sum", [P, 1])
        w_den = sb("w_den", [P, 1])
        w_inv = sb("w_inv", [P, 1])
        w_tok = sb("w_tok", [P, NT, E])
        wT = sb("wT", [E, S])
        w_raw = sb("w_raw", [P, UNROLL, 3 * P])
        gu_hi = sb("gu_hi", [P, 2, 2 * P], F32R)
        gu_lo = sb("gu_lo", [P, 2, 2 * P], F32R)
        dn_hi = sb("dn_hi", [P, 2, P], F32R)
        dn_lo = sb("dn_lo", [P, 2, P], F32R)
        w_spread = sb("w_spread", [P, UNROLL, S])
        act_g = sb("act_g", [P, 2, HALF])
        gated = sb("gated", [P, 2, HALF])
        hid = sb("hid", [P, 2, HALF])
        hid_hi = sb("hid_hi", [P, 2, HALF], F32R)
        hid_lo = sb("hid_lo", [P, 2, HALF], F32R)
        yT = sb("yT", [P, NH, HALF])
        bn2 = sb("bn2", [P, NT, 6])
        mv2 = sb("mv2", [P, NT, 2])
        var_eps2 = sb("var_eps2", [P, NT])
        rstd2 = sb("rstd2", [P, NT])
        y_out = sb("y_out", [P, NT, D])

        ps = ctx.enter_context(nc.psum_tensor("ps", [P, 8, HALF], F32))
        SCORES = (0, 2)
        TURN = (4, 5)
        PV, PROJ = 6, 7
        GATE, UP, SUM = (0, 1), (2, 3), (6, 7)

        PER, FIRST, sem = {}, {}, {}

        def signal(name, per, first=0):
            PER[name], FIRST[name] = per, first
            sem[name] = ctx.enter_context(nc.semaphore(name))

        for name in ("const_in", "const_dve", "brow_ps", "brow_sb"):
            signal(name, 0)
        signal("x_in", 16)
        for name, per in dict(
            xT_ps=2, xT_a=1, xT_d=1, q_ps=2, k_ps=2, v_ps=2, q_hi=2, k_hi=2, v_hi_sb=2, q_lo=2, k_lo=2, v_lo_sb=2, xb_sb=1,
            score_ps=NT, max_sb=NT, probs_sb=NT, pT_ps=2 * NT, pT_hi_sb=2 * NT, pT_lo_sb=2 * NT,
            pv_ps=NH, oT_sb=NH, proj_ps=NH, inv_sb=NH, res_sb=NT, bn_sb=NT, mv_sb=NT, ve_sb=NH, rstd_sb=NH, x1_sb=NT,
            x1T_ps=2, x1T_sb=2, x1T_hi_sb=2, x1T_lo_sb=2, logit_ps=1, exp_sb=1, w_ready=NT, wT_ps=2, wT_sb=2,
            gu_hi_sb=QP, gu_lo_sb=QP, dn_hi_sb=QP, dn_lo_sb=QP, gu_ps=STEPS, silu_sb=STEPS, m1_sb=STEPS, m2_sb=STEPS,
            hid_hi_sb=STEPS, hid_lo_sb=STEPS, dn_ps=STEPS,
            yT_sb=NH, yt_ps=NH, bn2_sb=NT, mv2_sb=NT, ve2_sb=NH, rstd2_sb=NH,
        ).items():
            signal(name, per)
        signal("y_sb", NT, first=1)
        signal("held", 0)
        signal("wT_out", 16)
        for k in range(UNROLL):
            signal(f"w_in{k}", 16 * (PAIRS // UNROLL) + 16 * (k == 0))
            signal(f"spread_in{k}", 32 * (PAIRS // UNROLL))
        signal("out_done", 16 * NH)
        DVE_ROUTE = 30
        signal("route", DVE_ROUTE * NT)

        def upto(name, b, k):
            return sem[name], b * PER[name] + k + FIRST[name]

        def cols(bank, t):
            return ps[:, bank, t * P:(t + 1) * P]

        def tile(m, t):
            return m[:, t * P:(t + 1) * P]

        def half(m, h):
            return m[:, h * HALF:(h + 1) * HALF]

        def split3(to, lhs, rhs, start=True, stop=True):
            nc.tensor.matmul(to, lhs[0], rhs[0], start=start, stop=False)
            nc.tensor.matmul(to, lhs[0], rhs[1], start=False, stop=False)
            return nc.tensor.matmul(to, lhs[1], rhs[0], start=False, stop=stop)

        def hold(engine):
            engine.sem_inc(sem["held"], 1)

        block = ctx.enter_context(nc.Block())
        N_CONST = 10

        @block.sync
        def _(sp):
            for dst, src in ((ident, ident_in), (wq, w_qkvo[0]), (wk, w_qkvo[1]), (wv, w_qkvo[2]), (wo, w_qkvo[3]), (gwT, gate_wT)):
                sp.dma_start(dst[:, :], src).then_inc(sem["const_in"], 16)
            with nc.allow_non_contiguous_dma(reason="four short bias columns"):
                sp.dma_start(bias_cols[:, :], b_qkvo.rearrange("n d -> d n")).then_inc(sem["const_in"], 16)
            sp.dma_start(lower[:, :, :].rearrange("p a b -> p (a b)"), lower_in.to_broadcast([P, GROUPS * GROUPS])).then_inc(sem["const_in"], 16)
            sp.dma_start(gbias[:, :], gate_bias.to_broadcast([P, E])).then_inc(sem["const_in"], 16)
            sp.dma_start(bo_row[:, :], b_qkvo[3:4, :].to_broadcast([P, D])).then_inc(sem["const_in"], 16)

            def load_pair(b, q, slot):
                sp.dma_start(w_raw[:, slot, :], w_pairs[q, :, :]).then_inc(sem[f"w_in{slot}"], 16)

            def load_spread(b, q, slot):
                for k in range(2):
                    row = w_scratch[b, 2 * q - 2 + k, :].rearrange("(o s) -> o s", o=1)
                    sp.dma_start(w_spread[k * F:(k + 1) * F, slot, :], row.to_broadcast([F, S])).then_inc(sem[f"spread_in{slot}"], 16)

            with sp.Fori(0, B) as b:
                sp.wait_ge(*upto("y_sb", b, 0))
                for q in range(UNROLL):
                    load_pair(b, q, q)
                sp.wait_ge(*upto("wT_out", b, 16))
                for q in range(1, UNROLL):
                    load_spread(b, q, q)
                with sp.Fori(0, PAIRS // UNROLL - 1) as i:
                    for k in range(UNROLL):
                        q = UNROLL * i + UNROLL + k
                        sp.wait_ge(*upto("dn_hi_sb", b, q - UNROLL + 1))
                        sp.wait_ge(*upto("dn_lo_sb", b, q - UNROLL + 1))
                        load_pair(b, q, k)
                        sp.wait_ge(*upto("m2_sb", b, NH * (q - UNROLL + 1)))
                        load_spread(b, q, k)
                q = PAIRS
                sp.wait_ge(*upto("dn_hi_sb", b, q - UNROLL + 1))
                sp.wait_ge(*upto("dn_lo_sb", b, q - UNROLL + 1))
                load_pair(b, q, 0)
                sp.wait_ge(*upto("m2_sb", b, NH * (q - UNROLL + 1)))
                load_spread(b, q, 0)

        @block.tensor
        def _(pe):
            pe.wait_ge(sem["const_in"], 16 * N_CONST)
            pe.wait_ge(sem["const_dve"], 4)
            nc.tensor.matmul(cols(PROJ, 0), bv_spread[:, :], wo[:, :], start=True, stop=True).then_inc(sem["brow_ps"], 1)

            def attention(b):
                pe.wait_ge(*upto("x_in", b, 16))
                pe.wait_ge(*upto("y_sb", b, 0))
                for h in range(NH):
                    for t in range(TPH):
                        mm = nc.tensor.transpose(cols(TURN[h], t), x_tok[:, TPH * h + t, :], ident[:, :])
                    mm.then_inc(sem["xT_ps"], 1)
                for h in range(NH):
                    pe.wait_ge(*upto(("xT_a", "xT_d")[h], b, 1))
                    nc.tensor.matmul(ps[:, SCORES[0] + h, :], wq_s[:, :], half(xT, h), start=True, stop=True).then_inc(sem["q_ps"], 1)
                    nc.tensor.matmul(ps[:, SCORES[1] + h, :], wk[:, :], half(xT, h), start=True, stop=True).then_inc(sem["k_ps"], 1)
                for h in range(NH):
                    for t in range(TPH):
                        mm = nc.tensor.matmul(cols(TURN[h], t), tile(xT, TPH * h + t), wv[:, :], start=True, stop=True)
                    mm.then_inc(sem["v_ps"], 1)

                def scores(j):
                    if j == 0:
                        for n in ("q_hi", "q_lo", "k_hi", "k_lo"):
                            pe.wait_ge(*upto(n, b, 2))
                    if j >= 2:
                        pe.wait_ge(*upto("probs_sb", b, j - 1))
                    for h in range(NH):
                        mm = split3(ps[:, SCORES[j % 2] + h, :], (tile(qT_hi, j), tile(qT_lo, j)), (half(kT_hi, h), half(kT_lo, h)))
                    mm.then_inc(sem["score_ps"], 1)

                def turn_probs(j):
                    pe.wait_ge(*upto("probs_sb", b, j + 1))
                    for h in range(NH):
                        if j == 0:
                            pe.wait_ge(*upto("v_lo_sb", b, h + 1))
                        else:
                            pe.wait_ge(*upto("pT_lo_sb", b, 2 * j - 1 + h))
                        for t in range(TPH):
                            mm = nc.tensor.transpose(cols(TURN[h], t), probs[:, j % 2, (TPH * h + t) * P:(TPH * h + t + 1) * P], ident[:, :])
                        mm.then_inc(sem["pT_ps"], 1)

                def mix(h):
                    pe.wait_ge(*upto("pT_lo_sb", b, 2 * TPH * (h + 1)))
                    if h:
                        pe.wait_ge(*upto("oT_sb", b, h))
                    for t in range(NT):
                        mm = split3(ps[:, PV, :], (v_hi[:, t, :], v_lo[:, t, :]), (pT_hi[:, t, :], pT_lo[:, t, :]), start=(t == 0), stop=(t == NT - 1))
                    mm.then_inc(sem["pv_ps"], 1)

                def project(h):
                    pe.wait_ge(*upto("oT_sb", b, h + 1))
                    if h:
                        pe.wait_ge(*upto("res_sb", b, TPH * h))
                    for t in range(TPH):
                        mm = nc.tensor.matmul(cols(PROJ, t), tile(oT, t), wo[:, :], start=True, stop=True)
                    mm.then_inc(sem["proj_ps"], 1)

                scores(0)
                scores(1)
                for j in range(NT):
                    turn_probs(j)
                    if j + 2 < NT:
                        scores(j + 2)
                    if j == TPH - 1:
                        mix(0)
                    if j == TPH:
                        project(0)
                mix(1)
                project(1)

            def turn_x1(b):
                for h in range(NH):
                    pe.wait_ge(*upto("x1_sb", b, TPH * (h + 1)))
                    for t in range(TPH):
                        mm = nc.tensor.transpose(cols(TURN[h], t), x1[:, TPH * h + t, :], ident[:, :])
                    mm.then_inc(sem["x1T_ps"], 1)
                for h in range(NH):
                    pe.wait_ge(*upto("x1T_sb", b, h + 1))
                    for t in range(TPH):
                        k = TPH * h + t
                        mm = nc.tensor.matmul(ps[:, PROJ, k * E:(k + 1) * E], tile(x1T, k), gwT[:, :], start=True, stop=True)
                mm.then_inc(sem["logit_ps"], 1)

            def turn_weights(b):
                for h in range(NH):
                    pe.wait_ge(*upto("w_ready", b, TPH * (h + 1)))
                    pe.wait_ge(*upto("x1T_lo_sb", b, h + 1))
                    hold(pe)
                    for t in range(TPH):
                        mm = nc.tensor.transpose(ps[0:E, TURN[h], t * P:(t + 1) * P], w_tok[:, TPH * h + t, :], ident[:, :])
                    mm.then_inc(sem["wT_ps"], 1)

            def experts(b):
                def seed(c):
                    pe.wait_ge(*upto("x1T_hi_sb", b, c + 1))
                    pe.wait_ge(*upto("x1T_lo_sb", b, c + 1))
                    nc.tensor.matmul(ps[:, SUM[c], :], identr[:, :], half(x1T_hi, c), start=True, stop=False)
                    nc.tensor.matmul(ps[:, SUM[c], :], identr[:, :], half(x1T_lo, c), start=False, stop=False)

                def gate_up(q, slot, c):
                    if c == 0:
                        pe.wait_ge(*upto("gu_hi_sb", b, q + 1))
                        pe.wait_ge(*upto("gu_lo_sb", b, q + 1))
                    if not (isinstance(q, int) and q == 0):
                        pe.wait_ge(*upto("silu_sb", b, NH * q + c - 1))
                        pe.wait_ge(*upto("m1_sb", b, NH * q + c - 1))
                    rhs = (half(x1T_hi, c), half(x1T_lo, c))
                    split3(ps[:, GATE[c], :], (gu_hi[:, slot, 0:P], gu_lo[:, slot, 0:P]), rhs)
                    split3(ps[:, UP[c], :], (gu_hi[:, slot, P:2 * P], gu_lo[:, slot, P:2 * P]), rhs).then_inc(sem["gu_ps"], 1)

                def down(q, slot, c, stop=False):
                    if c == 0:
                        pe.wait_ge(*upto("dn_hi_sb", b, q + 1))
                        pe.wait_ge(*upto("dn_lo_sb", b, q + 1))
                    pe.wait_ge(*upto("hid_lo_sb", b, NH * q + c + 1))
                    split3(ps[:, SUM[c], :], (dn_hi[:, slot, :], dn_lo[:, slot, :]), (hid_hi[:, c, :], hid_lo[:, c, :]),
                           start=False, stop=stop).then_inc(sem["dn_ps"], 1)

                pe.wait_ge(*upto("exp_sb", b, 1))
                for c in range(NH):
                    seed(c)
                for c in range(NH):
                    gate_up(0, 0, c)
                with pe.Fori(0, PAIRS // UNROLL) as i:
                    for k in range(UNROLL):
                        q = UNROLL * i + 1 + k
                        for c in range(NH):
                            gate_up(q, (k + 1) % 2, c)
                        for c in range(NH):
                            down(q - 1, k % 2, c)
                for c in range(NH):
                    down(PAIRS, PAIRS % 2, c, stop=True)
                for c in range(NH):
                    pe.wait_ge(*upto("yT_sb", b, c + 1))
                    for t in range(TPH):
                        mm = nc.tensor.transpose(cols(TURN[c], t), yT[:, c, t * P:(t + 1) * P], ident[:, :])
                    mm.then_inc(sem["yt_ps"], 1)

            with pe.Fori(0, B) as b:
                attention(b)
                turn_x1(b)
                turn_weights(b)
                experts(b)

        @block.scalar
        def _(act):
            act.wait_ge(sem["const_in"], 16 * N_CONST)
            act.wait_ge(sem["const_dve"], 4)

            def copy(to, of):
                return nc.scalar.activation(to, of, ACT.Copy)

            def attention(b):
                act.wait_ge(*upto("xT_ps", b, 1))
                copy(half(xT, 0), ps[:, TURN[0], :]).then_inc(sem["xT_a"], 1)
                for h in range(NH):
                    act.wait_ge(*upto("q_ps", b, h + 1))
                    nc.scalar.activation(half(qT_hi, h), ps[:, SCORES[0] + h, :], ACT.Identity, bias=bq_s[:, 0:1]).then_inc(sem["q_hi"], 1)
                    act.wait_ge(*upto("k_ps", b, h + 1))
                    nc.scalar.activation(half(kT_hi, h), ps[:, SCORES[1] + h, :], ACT.Identity, bias=bias_cols[:, 1:2]).then_inc(sem["k_hi"], 1)
                for h in range(NH):
                    act.wait_ge(*upto("v_ps", b, h + 1))
                    copy(v_hi[:, TPH * h:TPH * (h + 1), :].rearrange("p t d -> p (t d)"), ps[:, TURN[h], :]).then_inc(sem["v_hi_sb"], 1)

                def exps(j):
                    act.wait_ge(*upto("max_sb", b, j + 1))
                    if j >= 2:
                        act.wait_ge(*upto("pT_ps", b, 2 * (j - 1)))
                    nc.scalar.activation(probs[:, j % 2, :], ps[:, SCORES[j % 2]:SCORES[j % 2] + 2, :].rearrange("p a b -> p (a b)"),
                                         ACT.Exp, bias=neg_max[:, j:j + 1], accum_out=row_sum[:, j:j + 1]).then_inc(sem["probs_sb"], 1)

                def probs_hi(j):
                    for h in range(NH):
                        act.wait_ge(*upto("pT_ps", b, 2 * j + h + 1))
                        if j == TPH:
                            act.wait_ge(*upto("pv_ps", b, 1))
                        copy(pT_hi[:, TPH * h:TPH * (h + 1), (j % TPH) * P:(j % TPH + 1) * P],
                             ps[:, TURN[h], :].rearrange("p (t d) -> p t d", d=P)).then_inc(sem["pT_hi_sb"], 1)

                def out_turned(h):
                    act.wait_ge(*upto("pv_ps", b, h + 1))
                    if h:
                        act.wait_ge(*upto("proj_ps", b, h))
                    copy(oT[:, :], ps[:, PV, :]).then_inc(sem["oT_sb"], 1)

                exps(0)
                for j in range(NT):
                    if j + 1 < NT:
                        exps(j + 1)
                    if j == TPH:
                        out_turned(0)
                    probs_hi(j)
                out_turned(1)

            def turned_x1(b):
                for h in range(NH):
                    act.wait_ge(*upto("x1T_ps", b, h + 1))
                    copy(half(x1T, h), ps[:, TURN[h], :]).then_inc(sem["x1T_sb"], 1)
                    copy(half(x1T_hi, h), ps[:, TURN[h], :]).then_inc(sem["x1T_hi_sb"], 1)
                act.wait_ge(*upto("logit_ps", b, 1))
                nc.scalar.activation(exp_neg[:, :, :].rearrange("p t e -> p (t e)"), ps[:, PROJ, :], ACT.Exp, scale=-1.0).then_inc(sem["exp_sb"], 1)

            def turned_weights(b):
                for h in range(NH):
                    act.wait_ge(*upto("wT_ps", b, h + 1))
                    copy(half(wT, h), ps[0:E, TURN[h], :]).then_inc(sem["wT_sb"], 1)

            def experts(b):
                def gu_split(q, raw, slot, loads):
                    act.wait_ge(sem[f"w_in{raw}"], b * PER[f"w_in{raw}"] + 16 * loads)
                    if not is_first_two(q):
                        act.wait_ge(*upto("gu_ps", b, NH * (q - 1)))
                    copy(gu_hi[:, slot, :], w_raw[:, raw, 0:2 * P]).then_inc(sem["gu_hi_sb"], 1)

                def dn_split(q, raw, slot):
                    if not is_first_two(q):
                        act.wait_ge(*upto("dn_ps", b, NH * (q - 1)))
                    copy(dn_hi[:, slot, :], w_raw[:, raw, 2 * P:3 * P]).then_inc(sem["dn_hi_sb"], 1)

                def silu(q, c):
                    act.wait_ge(*upto("gu_ps", b, NH * q + c + 1))
                    if not is_shared(q):
                        act.wait_ge(*upto("m1_sb", b, NH * q + c - 1))
                    nc.scalar.activation(act_g[:, c, :], ps[:, GATE[c], :], ACT.Silu).then_inc(sem["silu_sb"], 1)

                act.wait_ge(*upto("y_sb", b, 0))
                gu_split(0, 0, 0, 1)
                dn_split(0, 0, 0)
                silu(0, 0)
                silu(0, 1)
                gu_split(1, 1, 1, 1)

                def body(i, last=False):
                    for k in range(UNROLL):
                        q = UNROLL * i + 1 + k
                        if not (last and k == UNROLL - 1):
                            gu_split(q + 1, (k + 2) % UNROLL, k % 2, i + (1 if k + 2 < UNROLL else 2))
                        dn_split(q, (k + 1) % UNROLL, (k + 1) % 2)
                        silu(q, 0)
                        silu(q, 1)

                with act.Fori(0, PAIRS // UNROLL - 1) as i:
                    body(i)
                body(PAIRS // UNROLL - 1, last=True)
                for c in range(NH):
                    act.wait_ge(*upto("dn_ps", b, STEPS - 1 + c))
                    copy(yT[:, c, :], ps[:, SUM[c], :]).then_inc(sem["yT_sb"], 1)

            with act.Fori(0, B) as b:
                attention(b)
                turned_x1(b)
                turned_weights(b)
                experts(b)

        @block.gpsimd
        def _(gp):
            gp.wait_ge(sem["brow_sb"], 1)

            def power(to, of):
                return nc.gpsimd.tensor_tensor(to, of, minus_half[:, :], ALU.pow)

            def subtract(to, a, hi):
                return nc.gpsimd.tensor_tensor(to, a, hi.bitcast(F32), ALU.subtract)

            def experts(b):
                def gu_split(q, raw, slot):
                    gp.wait_ge(*upto("gu_hi_sb", b, q + 1))
                    subtract(gu_lo[:, slot, :], w_raw[:, raw, 0:2 * P], gu_hi[:, slot, :]).then_inc(sem["gu_lo_sb"], 1)

                def dn_split(q, raw, slot):
                    gp.wait_ge(*upto("dn_hi_sb", b, q + 1))
                    subtract(dn_lo[:, slot, :], w_raw[:, raw, 2 * P:3 * P], dn_hi[:, slot, :]).then_inc(sem["dn_lo_sb"], 1)

                def hid_split(q, c):
                    gp.wait_ge(*upto("hid_hi_sb", b, NH * q + c + 1))
                    subtract(hid_lo[:, c, :], hid[:, c, :], hid_hi[:, c, :]).then_inc(sem["hid_lo_sb"], 1)

                gu_split(0, 0, 0)
                dn_split(0, 0, 0)
                hid_split(0, 0)
                gu_split(1, 1, 1)
                hid_split(0, 1)

                def body(i, last=False):
                    for k in range(UNROLL):
                        q = UNROLL * i + 1 + k
                        if not (last and k == UNROLL - 1):
                            gu_split(q + 1, (k + 2) % UNROLL, k % 2)
                        dn_split(q, (k + 1) % UNROLL, (k + 1) % 2)
                        hid_split(q, 0)
                        hid_split(q, 1)

                with gp.Fori(0, PAIRS // UNROLL - 1) as i:
                    body(i)
                body(PAIRS // UNROLL - 1, last=True)

            with gp.Fori(0, B) as b:
                gp.wait_ge(*upto("y_sb", b, 0))
                hold(gp)
                gp.dma_start(x_tok[:, :, :], x[b, :, :].rearrange("(t p) d -> p t d", p=P)).then_inc(sem["x_in"], 16)
                gp.wait_ge(*upto("x_in", b, 16))
                nc.gpsimd.tensor_tensor(x_b[:, :, :], x_tok[:, :, :], b_row[:, :].unsqueeze(1).to_broadcast([P, NT, D]), ALU.add).then_inc(sem["xb_sb"], 1)
                for h in range(NH):
                    gp.wait_ge(*upto("ve_sb", b, h + 1))
                    power(rstd[:, TPH * h:TPH * (h + 1)], var_eps[:, TPH * h:TPH * (h + 1)]).then_inc(sem["rstd_sb"], 1)
                gp.wait_ge(*upto("wT_sb", b, 2))
                hold(gp)
                gp.dma_start(w_scratch[b, :, :], wT[:, :]).then_inc(sem["wT_out"], 16)
                experts(b)
                for h in range(NH):
                    gp.wait_ge(*upto("ve2_sb", b, h + 1))
                    power(rstd2[:, TPH * h:TPH * (h + 1)], var_eps2[:, TPH * h:TPH * (h + 1)]).then_inc(sem["rstd2_sb"], 1)
                for h in range(NH):
                    gp.wait_ge(*upto("y_sb", b, TPH * (h + 1)))
                    hold(gp)
                    gp.dma_start(out[b, h * HALF:(h + 1) * HALF, :].rearrange("(t p) d -> p t d", p=P),
                                 y_out[:, TPH * h:TPH * (h + 1), :]).then_inc(sem["out_done"], 16)
            gp.wait_ge(sem["out_done"], 16 * B * NH)

        @block.vector
        def _(ve):
            nc.vector.memset(minus_half[:, :], -0.5).then_inc(sem["y_sb"], 1)
            ve.wait_ge(sem["const_in"], 16 * N_CONST)
            nc.vector.tensor_copy(bv_spread[:, :], bias_cols[:, 2:3].to_broadcast([P, P])).then_inc(sem["const_dve"], 1)
            nc.vector.tensor_copy(identr[:, :], ident[:, :]).then_inc(sem["const_dve"], 1)
            nc.vector.tensor_scalar(wq_s[:, :], wq[:, :], SCALE, None, ALU.mult).then_inc(sem["const_dve"], 1)
            nc.vector.tensor_scalar(bq_s[:, :], bias_cols[:, 0:1], SCALE, None, ALU.mult).then_inc(sem["const_dve"], 1)
            ve.wait_ge(sem["brow_ps"], 1)
            nc.vector.tensor_tensor(b_row[:, :], cols(PROJ, 0), bo_row[:, :], ALU.add).then_inc(sem["brow_sb"], 1)

            def rest(to, of, bias, hi):
                return nc.vector.scalar_tensor_tensor(out=to, in0=of, scalar=bias, in1=hi.bitcast(F32), op0=ALU.add, op1=ALU.subtract)

            def attention(b):
                ve.wait_ge(*upto("xT_ps", b, 2))
                nc.vector.tensor_copy(half(xT, 1), ps[:, TURN[1], :]).then_inc(sem["xT_d"], 1)
                for h in range(NH):
                    ve.wait_ge(*upto("q_hi", b, h + 1))
                    rest(half(qT_lo, h), ps[:, SCORES[0] + h, :], bq_s[:, 0:1], half(qT_hi, h)).then_inc(sem["q_lo"], 1)
                    ve.wait_ge(*upto("k_hi", b, h + 1))
                    rest(half(kT_lo, h), ps[:, SCORES[1] + h, :], bias_cols[:, 1:2], half(kT_hi, h)).then_inc(sem["k_lo"], 1)
                for h in range(NH):
                    ve.wait_ge(*upto("v_hi_sb", b, h + 1))
                    nc.vector.tensor_tensor(v_lo[:, TPH * h:TPH * (h + 1), :].rearrange("p t d -> p (t d)"), ps[:, TURN[h], :],
                                            v_hi[:, TPH * h:TPH * (h + 1), :].rearrange("p t d -> p (t d)").bitcast(F32),
                                            ALU.subtract).then_inc(sem["v_lo_sb"], 1)

                def row_max(j):
                    ve.wait_ge(*upto("score_ps", b, j + 1))
                    nc.vector.tensor_reduce(neg_max[:, j:j + 1], ps[:, SCORES[j % 2]:SCORES[j % 2] + 2, :].rearrange("p a b -> p (a b)"),
                                            AX.X, ALU.max, negate=True).then_inc(sem["max_sb"], 1)

                def probs_lo(j):
                    at = slice((j % TPH) * P, (j % TPH + 1) * P)
                    for h in range(NH):
                        ve.wait_ge(*upto("pT_hi_sb", b, 2 * j + h + 1))
                        nc.vector.tensor_tensor(pT_lo[:, TPH * h:TPH * (h + 1), at], ps[:, TURN[h], :].rearrange("p (t d) -> p t d", d=P),
                                                pT_hi[:, TPH * h:TPH * (h + 1), at].bitcast(F32), ALU.subtract).then_inc(sem["pT_lo_sb"], 1)

                def residual_norm(h):
                    tiles = range(TPH * h, TPH * (h + 1))
                    quad = slice(TPH * h, TPH * (h + 1))
                    ve.wait_ge(*upto("probs_sb", b, TPH * (h + 1)))
                    nc.vector.reciprocal(inv_sum[:, quad], row_sum[:, quad]).then_inc(sem["inv_sb"], 1)
                    ve.wait_ge(*upto("inv_sb", b, h + 1))
                    ve.wait_ge(*upto("proj_ps", b, h + 1))
                    ve.wait_ge(*upto("xb_sb", b, 1))
                    for j in tiles:
                        nc.vector.scalar_tensor_tensor(out=x_res[:, j, :], in0=cols(PROJ, j % TPH), scalar=inv_sum[:, j:j + 1],
                                                       in1=x_b[:, j, :], op0=ALU.mult, op1=ALU.add).then_inc(sem["res_sb"], 1)
                    for j in tiles:
                        ve.wait_ge(*upto("res_sb", b, j + 1))
                        nc.vector.bn_stats(bn[:, j, :], x_res[:, j, :]).then_inc(sem["bn_sb"], 1)
                    for j in tiles:
                        ve.wait_ge(*upto("bn_sb", b, j + 1))
                        hold(ve)
                        nc.vector.bn_aggr(mv[:, j, :], bn[:, j, :]).then_inc(sem["mv_sb"], 1)
                    ve.wait_ge(*upto("mv_sb", b, TPH * (h + 1)))
                    nc.vector.tensor_scalar(var_eps[:, quad], mv[:, quad, 1], EPS, None, ALU.add).then_inc(sem["ve_sb"], 1)

                def normalise(h):
                    ve.wait_ge(*upto("rstd_sb", b, h + 1))
                    for j in range(TPH * h, TPH * (h + 1)):
                        nc.vector.tensor_scalar(x1[:, j, :], x_res[:, j, :], mv[:, j, 0:1], rstd[:, j:j + 1],
                                                ALU.subtract, ALU.mult).then_inc(sem["x1_sb"], 1)

                row_max(0)
                for j in range(NT):
                    if j + 1 < NT:
                        row_max(j + 1)
                    probs_lo(j)
                    if j == TPH + 1:
                        residual_norm(0)
                    if j == TPH + 2:
                        normalise(0)
                residual_norm(1)
                normalise(1)

            def turned_x1(b):
                for h in range(NH):
                    ve.wait_ge(*upto("x1T_hi_sb", b, h + 1))
                    nc.vector.tensor_tensor(half(x1T_lo, h), ps[:, TURN[h], :], half(x1T_hi, h).bitcast(F32), ALU.subtract).then_inc(sem["x1T_lo_sb"], 1)

            def route(b, j):
                links = 0

                def link(instruction):
                    nonlocal links
                    instruction.then_inc(sem["route"], 1)
                    links += 1
                    ve.wait_ge(*upto("route", b, j * DVE_ROUTE + links))

                v = nc.vector
                link(v.tensor_scalar(denom[:, :], exp_neg[:, j, :], 1.0, None, ALU.add))
                link(v.reciprocal(sig[:, :], denom[:, :]))
                link(v.tensor_tensor(biased[:, :, :].rearrange("p g e -> p (g e)"), sig[:, :], gbias[:, :], ALU.add))
                link(v.tensor_tensor(hi4[:, :, :], biased[:, :, 0:4], biased[:, :, 4:8], ALU.max))
                link(v.tensor_tensor(lo4[:, :, :], biased[:, :, 0:4], biased[:, :, 4:8], ALU.min))
                for hi_a, lo_a, hi_b, lo_b, mn, mx, w in ((hi4, lo4, hi2, lo2, mn2, mx2, 2), (hi2, lo2, hi1, lo1, mn1, mx1, 1)):
                    link(v.tensor_tensor(hi_b[:, :, :], hi_a[:, :, 0:w], hi_a[:, :, w:2 * w], ALU.max))
                    link(v.tensor_tensor(mn[:, :, :], hi_a[:, :, 0:w], hi_a[:, :, w:2 * w], ALU.min))
                    link(v.tensor_tensor(mx[:, :, :], lo_a[:, :, 0:w], lo_a[:, :, w:2 * w], ALU.max))
                    link(v.tensor_tensor(lo_b[:, :, :], mn[:, :, :], mx[:, :, :], ALU.max))
                link(v.tensor_tensor(g_score[:, :], hi1[:, :, 0], lo1[:, :, 0], ALU.add))
                other = g_score[:, :].unsqueeze(1).to_broadcast([P, GROUPS, GROUPS])
                own = g_score[:, :].unsqueeze(2).to_broadcast([P, GROUPS, GROUPS])
                link(v.tensor_tensor(beats[:, :, :], other, own, ALU.is_gt))
                link(v.tensor_tensor(ties[:, :, :], other, own, ALU.is_equal))
                link(v.tensor_tensor(ties_low[:, :, :], ties[:, :, :], lower[:, :, :], ALU.mult))
                link(v.tensor_tensor(beaten[:, :, :], beats[:, :, :], ties_low[:, :, :], ALU.add))
                link(v.tensor_reduce(rank[:, :], beaten[:, :, :], AX.X, ALU.add))
                link(v.tensor_scalar(g_in[:, :], rank[:, :], TOP_GROUPS - 0.5, None, ALU.is_lt))
                link(v.tensor_scalar(g_out[:, :], g_in[:, :], FAR, -FAR, ALU.mult, ALU.add))
                link(v.tensor_tensor(kept[:, :, :], biased[:, :, :], g_in[:, :].unsqueeze(2).to_broadcast([P, GROUPS, E // GROUPS]), ALU.mult))
                link(v.tensor_tensor(masked[:, :, :], kept[:, :, :], g_out[:, :].unsqueeze(2).to_broadcast([P, GROUPS, E // GROUPS]), ALU.add))
                flat = masked[:, :, :].rearrange("p g e -> p (g e)")
                hold(ve)
                link(v.max(top8[:, :], flat))
                hold(ve)
                link(v.match_replace(out=replaced[:, :], in_to_replace=top8[:, :], in_values=flat, imm_value=GONE))
                link(v.tensor_tensor(chosen[:, :], replaced[:, :], flat, ALU.not_equal))
                link(v.tensor_tensor(w_raw8[:, :], sig[:, :], chosen[:, :], ALU.mult))
                link(v.tensor_reduce(w_sum[:, :], w_raw8[:, :], AX.X, ALU.add))
                link(v.tensor_scalar(w_den[:, :], w_sum[:, :], 1e-20, None, ALU.add))
                link(v.reciprocal(w_inv[:, :], w_den[:, :]))
                v.tensor_scalar(w_tok[:, j, :], w_raw8[:, :], w_inv[:, 0:1], ROUTE_SCALE, ALU.mult, ALU.mult).then_inc(sem["w_ready"], 1)
                assert links == DVE_ROUTE

            def experts(b):
                def hidden(q, c, spread=None, loads=None):
                    n = NH * q + c
                    ve.wait_ge(*upto("silu_sb", b, n + 1))
                    if not is_shared(q):
                        ve.wait_ge(*upto("m2_sb", b, n - 1))
                    nc.vector.tensor_tensor(gated[:, c, :], act_g[:, c, :], ps[:, UP[c], :], ALU.mult).then_inc(sem["m1_sb"], 1)
                    ve.wait_ge(*upto("m1_sb", b, n + 1))
                    if not is_shared(q):
                        ve.wait_ge(*upto("hid_lo_sb", b, n - 1))
                        ve.wait_ge(sem[f"spread_in{spread}"], b * PER[f"spread_in{spread}"] + 32 * loads)
                        m2 = nc.vector.tensor_tensor(hid[:, c, :], gated[:, c, :], half(w_spread[:, spread, :], c), ALU.mult)
                    else:
                        m2 = nc.vector.tensor_copy(hid[:, c, :], gated[:, c, :])
                    m2.then_inc(sem["m2_sb"], 1)
                    ve.wait_ge(*upto("m2_sb", b, n + 1))
                    if not is_shared(q):
                        ve.wait_ge(*upto("dn_ps", b, n - 1))
                    nc.vector.tensor_copy(hid_hi[:, c, :], hid[:, c, :]).then_inc(sem["hid_hi_sb"], 1)

                hidden(0, 0)
                hidden(0, 1)
                with ve.Fori(0, PAIRS // UNROLL) as i:
                    for k in range(UNROLL):
                        for c in range(NH):
                            hidden(UNROLL * i + 1 + k, c, (k + 1) % UNROLL, i + 1)

                for h in range(NH):
                    quad = slice(TPH * h, TPH * (h + 1))
                    ve.wait_ge(*upto("yt_ps", b, h + 1))
                    for t in range(TPH):
                        nc.vector.bn_stats(bn2[:, TPH * h + t, :], cols(TURN[h], t)).then_inc(sem["bn2_sb"], 1)
                    for t in range(TPH):
                        j = TPH * h + t
                        ve.wait_ge(*upto("bn2_sb", b, j + 1))
                        hold(ve)
                        nc.vector.bn_aggr(mv2[:, j, :], bn2[:, j, :]).then_inc(sem["mv2_sb"], 1)
                    ve.wait_ge(*upto("mv2_sb", b, TPH * (h + 1)))
                    nc.vector.tensor_scalar(var_eps2[:, quad], mv2[:, quad, 1], EPS, None, ALU.add).then_inc(sem["ve2_sb"], 1)
                for h in range(NH):
                    ve.wait_ge(*upto("rstd2_sb", b, h + 1))
                    for t in range(TPH):
                        j = TPH * h + t
                        nc.vector.tensor_scalar(y_out[:, j, :], cols(TURN[h], t), mv2[:, j, 0:1], rstd2[:, j:j + 1],
                                                ALU.subtract, ALU.mult).then_inc(sem["y_sb"], 1)

            with ve.Fori(0, B) as b:
                attention(b)
                turned_x1(b)
                ve.wait_ge(*upto("exp_sb", b, 1))
                hold(ve)
                with ve.Fori(0, NT) as j:
                    route(b, j)
                experts(b)


def is_shared(q):
    return isinstance(q, int) and q == 0


def is_first_two(q):
    return isinstance(q, int) and q < 2


def kernel(**inputs):
    import numpy as np
    import concourse.bacc as bacc
    from concourse.bass_utils import run_bass_kernel_spmd

    a = {k: np.asarray(v) for k, v in inputs.items()}
    x = np.ascontiguousarray(a["L0_attn_x"])
    B, S, D = x.shape
    E, _, F = a["L0_ffn_We_gate"].shape

    def pairs(routed, shared, axis):
        all_ = np.concatenate([shared[None], np.zeros_like(shared)[None], routed])
        return np.concatenate([all_[0::2], all_[1::2]], axis=axis)

    w_pairs = np.concatenate([
        pairs(a["L0_ffn_We_gate"], a["L0_ffn_Ws_gate"], 2),
        pairs(a["L0_ffn_We_up"], a["L0_ffn_Ws_up"], 2),
        pairs(a["L0_ffn_We_down"], a["L0_ffn_Ws_down"], 1),
    ], axis=2)
    arrays = {
        "x": x,
        "w_qkvo": np.stack([a[f"L0_attn_W{i}"] for i in (1, 2, 3, 4)]),
        "b_qkvo": np.stack([a[f"L0_attn_b{i}"] for i in (1, 2, 3, 4)]),
        "gate_wT": np.ascontiguousarray(a["L0_ffn_gate_w"].T),
        "gate_bias": a["L0_ffn_gate_bias"][None],
        "w_pairs": np.ascontiguousarray(w_pairs),
        "ident_in": np.eye(P, dtype=np.float32),
        "lower_in": np.tril(np.ones((8, 8), np.float32), -1).reshape(1, -1),
    }
    nc = bacc.Bacc("TRN2", target_bir_lowering=False, num_devices=1)
    args = [nc.dram_tensor(n, v.shape, mybir.dt.from_np(v.dtype), kind="ExternalInput").ap() for n, v in arrays.items()]
    args.append(nc.dram_tensor("w_scratch", (B, E, S), F32, kind="Internal").ap())
    args.append(nc.dram_tensor("out", x.shape, F32, kind="ExternalOutput").ap())
    block_kernel(nc, *args)
    r = run_bass_kernel_spmd(nc, [arrays], core_ids=[0])
    return r.results[0]["out"]
```

```python
from contextlib import ExitStack

import concourse.bass as bass
from concourse import mybir

F32 = mybir.dt.float32
F32R = mybir.dt.float32r
ALU = mybir.AluOpType
ACT = mybir.ActivationFunctionType
AX = mybir.AxisListType

P = 128
HALF = 512
EPS = 1e-5
ROUTE_SCALE = 2.5
TOP_GROUPS = 4
FAR = 1e30
GONE = -3e38
UNROLL = 4


def block_kernel(nc, x, w_qkvo, b_qkvo, gate_wT, gate_bias, w_pairs, ident_in, lower_in, w_scratch, out):
    B, S, D = x.shape
    E = gate_wT.shape[1]
    F = P // 2
    GROUPS = 8
    PER_GROUP = E // GROUPS
    NT = S // P
    NH = S // HALF
    TPH = HALF // P
    PAIRS = E // 2
    QP = PAIRS + 1
    STEPS = QP * NH
    SCALE = float(D) ** -0.5
    assert D == P and NH == 2 and E == 64 and w_pairs.shape[0] == QP and PAIRS % UNROLL == 0

    ctx = ExitStack()
    with ctx:
        def sb(name, shape, dt=F32):
            return ctx.enter_context(nc.sbuf_tensor(name, shape, dt))

        ident = sb("ident", [P, P])
        identr = sb("identr", [P, P], F32R)
        lower = sb("lower", [P, GROUPS, GROUPS])
        wq, wk, wv, wo = (sb(n, [P, P]) for n in ("wq", "wk", "wv", "wo"))
        wq_s = sb("wq_s", [P, P])
        bq_s = sb("bq_s", [P, 1])
        bias_cols = sb("bias_cols", [P, 4])
        bo_row = sb("bo_row", [P, P])
        bv_spread = sb("bv_spread", [P, P])
        b_row = sb("b_row", [P, P])
        gwT = sb("gwT", [P, E])
        gbias = sb("gbias", [P, E])
        minus_half = sb("minus_half", [P, TPH])
        x_tok = sb("x_tok", [P, NT, D])
        xT = sb("xT", [P, S])
        qT_hi, qT_lo, kT_hi, kT_lo = (sb(n, [P, S], F32R) for n in ("qT_hi", "qT_lo", "kT_hi", "kT_lo"))
        v_hi = sb("v_hi", [P, NT, D], F32R)
        v_lo = sb("v_lo", [P, NT, D], F32R)
        neg_max = sb("neg_max", [P, NT])
        row_sum = sb("row_sum", [P, NT])
        inv_sum = sb("inv_sum", [P, NT])
        probs = sb("probs", [P, 2, S])
        pT_hi = sb("pT_hi", [P, 2, NT, 2 * P], F32R)
        pT_lo = sb("pT_lo", [P, 2, NT, 2 * P], F32R)
        oT = sb("oT", [P, 2, 2 * P])
        x_b = sb("x_b", [P, NT, D])
        x_res = sb("x_res", [P, NT, D])
        x1 = sb("x1", [P, NT, D])
        bn = sb("bn", [P, NT, 6])
        mv = sb("mv", [P, NT, 2])
        var_eps = sb("var_eps", [P, NT])
        rstd = sb("rstd", [P, NT])
        x1T = sb("x1T", [P, S])
        x1T_hi = sb("x1T_hi", [P, 2, S], F32R)
        x1T_lo = sb("x1T_lo", [P, 2, S], F32R)
        exp_neg = sb("exp_neg", [P, NT, E])
        denom = sb("denom", [P, NT, E])
        sig = sb("sig", [P, NT, E])
        biased = sb("biased", [P, NT, GROUPS, PER_GROUP])
        hi4, lo4 = (sb(n, [P, NT, GROUPS, 4]) for n in ("hi4", "lo4"))
        hi2, lo2, mn2, mx2 = (sb(n, [P, NT, GROUPS, 2]) for n in ("hi2", "lo2", "mn2", "mx2"))
        hi1, lo1, mn1, mx1 = (sb(n, [P, NT, GROUPS, 1]) for n in ("hi1", "lo1", "mn1", "mx1"))
        g_score = sb("g_score", [P, NT, GROUPS])
        beats, ties, beaten = (sb(n, [P, NT, GROUPS, GROUPS]) for n in ("beats", "ties", "beaten"))
        rank, g_in, g_out = (sb(n, [P, NT, GROUPS]) for n in ("rank", "g_in", "g_out"))
        kept, masked = (sb(n, [P, NT, GROUPS, PER_GROUP]) for n in ("kept", "masked"))
        top8 = sb("top8", [P, NT, 8])
        replaced, chosen, w_raw8 = (sb(n, [P, NT, E]) for n in ("replaced", "chosen", "w_raw8"))
        w_sum, w_den, w_inv = (sb(n, [P, NT]) for n in ("w_sum", "w_den", "w_inv"))
        w_tok = sb("w_tok", [P, NT, E])
        wT = sb("wT", [E, S])
        w_raw = sb("w_raw", [P, UNROLL, 3 * P])
        gu_hi = sb("gu_hi", [P, 2, 2 * P], F32R)
        gu_lo = sb("gu_lo", [P, 2, 2 * P], F32R)
        dn_hi = sb("dn_hi", [P, 2, P], F32R)
        dn_lo = sb("dn_lo", [P, 2, P], F32R)
        w_spread = sb("w_spread", [P, UNROLL, S])
        act_g = sb("act_g", [P, 2, HALF])
        gated = sb("gated", [P, 2, HALF])
        hid = sb("hid", [P, 2, HALF])
        hid_hi = sb("hid_hi", [P, 2, HALF], F32R)
        hid_lo = sb("hid_lo", [P, 2, HALF], F32R)
        yT = sb("yT", [P, NH, HALF])
        bn2 = sb("bn2", [P, NT, 6])
        mv2 = sb("mv2", [P, NT, 2])
        var_eps2 = sb("var_eps2", [P, NT])
        rstd2 = sb("rstd2", [P, NT])
        y_out = sb("y_out", [P, NT, D])

        ps = ctx.enter_context(nc.psum_tensor("ps", [P, 8, HALF], F32))
        SCORES = (0, 2)
        TURN = (4, 5)
        PV, PROJ = 6, 7
        GATE, UP, SUM = (0, 1), (2, 3), (6, 7)

        PER, FIRST, sem = {}, {}, {}
        ROUTED_AT_ONCE = 2

        def signal(name, per, first=0):
            PER[name], FIRST[name] = per, first
            sem[name] = ctx.enter_context(nc.semaphore(name))

        for name in ("const_in", "const_dve", "brow_ps", "brow_sb"):
            signal(name, 0)
        signal("x_in", 16)
        for name, per in dict(
            xT_ps=2, xT_a=1, xT_d=1, q_ps=2, k_ps=2, v_ps=2, q_hi=2, k_hi=2, v_hi_sb=2, q_lo=2, k_lo=2, v_lo_sb=2, xb_sb=1,
            score_ps=NT, max_sb=NT, probs_sb=NT, pT_ps=2 * NT, pT_hi_sb=2 * NT, pT_lo_sb=2 * NT,
            pv_ps=NT // 2, oT_sb=NT // 2, proj_ps=NT // 2, inv_sb=NT // 2, res_sb=NT, bn_sb=NT, mv_sb=NT, ve_sb=NH, rstd_sb=NH, x1_sb=NT,
            x1T_ps=2, x1T_sb=2, x1T_hi_sb=2, x1T_lo_sb=2, logit_ps=1, exp_sb=1, w_ready=NT // ROUTED_AT_ONCE, wT_ps=2, wT_sb=2,
            gu_hi_sb=QP, gu_lo_sb=QP, dn_hi_sb=QP, dn_lo_sb=QP, gu_ps=STEPS, silu_sb=STEPS, m1_sb=STEPS, m2_sb=STEPS,
            hid_hi_sb=STEPS, hid_lo_sb=STEPS, dn_ps=STEPS,
            yT_sb=NH, yt_ps=NH, bn2_sb=NT, mv2_sb=NT, ve2_sb=NH, rstd2_sb=NH,
        ).items():
            signal(name, per)
        signal("y_sb", NT, first=1)
        signal("held", 0)
        signal("wT_out", 16)
        for k in range(UNROLL):
            signal(f"w_in{k}", 16 * (PAIRS // UNROLL) + 16 * (k == 0))
            signal(f"spread_in{k}", 32 * (PAIRS // UNROLL))
        signal("out_done", 16 * NH)
        SIGMOID, CHOOSE = 3, 26 + 2 * ROUTED_AT_ONCE
        for name in ("route0", "w_ready0", "sigmoid", "choose"):
            signal(name, 0)

        def upto(name, b, k):
            return sem[name], b * PER[name] + k + FIRST[name]

        def cols(bank, t):
            return ps[:, bank, t * P:(t + 1) * P]

        def tile(m, t):
            return m[:, t * P:(t + 1) * P]

        def half(m, h):
            return m[:, h * HALF:(h + 1) * HALF]

        def split3(to, lhs, rhs, start=True, stop=True):
            nc.tensor.matmul(to, lhs[0], rhs[0], start=start, stop=False)
            nc.tensor.matmul(to, lhs[0], rhs[1], start=False, stop=False)
            return nc.tensor.matmul(to, lhs[1], rhs[0], start=False, stop=stop)

        def hold(engine):
            engine.sem_inc(sem["held"], 1)

        block = ctx.enter_context(nc.Block())
        N_CONST = 10

        @block.sync
        def _(sp):
            for dst, src in ((ident, ident_in), (wq, w_qkvo[0]), (wk, w_qkvo[1]), (wv, w_qkvo[2]), (wo, w_qkvo[3]), (gwT, gate_wT)):
                sp.dma_start(dst[:, :], src).then_inc(sem["const_in"], 16)
            with nc.allow_non_contiguous_dma(reason="four short bias columns"):
                sp.dma_start(bias_cols[:, :], b_qkvo.rearrange("n d -> d n")).then_inc(sem["const_in"], 16)
            sp.dma_start(lower[:, :, :].rearrange("p a b -> p (a b)"), lower_in.to_broadcast([P, GROUPS * GROUPS])).then_inc(sem["const_in"], 16)
            sp.dma_start(gbias[:, :], gate_bias.to_broadcast([P, E])).then_inc(sem["const_in"], 16)
            sp.dma_start(bo_row[:, :], b_qkvo[3:4, :].to_broadcast([P, D])).then_inc(sem["const_in"], 16)

            def load_x(a):
                sp.dma_start(x_tok[:, :, :], x[a, :, :].rearrange("(t p) d -> p t d", p=P)).then_inc(sem["x_in"], 16)

            def load_pair(q, slot):
                sp.dma_start(w_raw[:, slot, :], w_pairs[q, :, :]).then_inc(sem[f"w_in{slot}"], 16)

            def load_spread(b, q, slot):
                for k in range(2):
                    row = w_scratch[b, 2 * q - 2 + k, :].rearrange("(o s) -> o s", o=1)
                    sp.dma_start(w_spread[k * F:(k + 1) * F, slot, :], row.to_broadcast([F, S])).then_inc(sem[f"spread_in{slot}"], 16)

            def refill(b, q, slot):
                sp.wait_ge(*upto("dn_hi_sb", b, q - UNROLL + 1))
                sp.wait_ge(*upto("gu_lo_sb", b, q - UNROLL + 1))
                sp.wait_ge(*upto("dn_lo_sb", b, q - UNROLL + 1))
                hold(sp)
                load_pair(q, slot)
                sp.wait_ge(*upto("m2_sb", b, NH * (q - UNROLL + 1)))
                hold(sp)
                load_spread(b, q, slot)

            def experts(b):
                sp.wait_ge(*upto("y_sb", b, 0))
                for q in range(UNROLL):
                    load_pair(q, q)
                sp.wait_ge(*upto("wT_out", b, 16))
                hold(sp)
                for q in range(1, UNROLL):
                    load_spread(b, q, q)
                with sp.Fori(0, PAIRS // UNROLL - 1) as i:
                    for k in range(UNROLL):
                        refill(b, UNROLL * i + UNROLL + k, k)
                refill(b, PAIRS, 0)

            load_x(0)
            with sp.Fori(0, B - 1) as b:
                sp.wait_ge(*upto("xT_ps", b, 2))
                hold(sp)
                sp.wait_ge(*upto("xb_sb", b, 1))
                hold(sp)
                load_x(b + 1)
                experts(b)
            experts(B - 1)

        @block.tensor
        def _(pe):
            pe.wait_ge(sem["const_in"], 16 * N_CONST)
            pe.wait_ge(sem["const_dve"], 4)
            nc.tensor.matmul(cols(PROJ, 0), bv_spread[:, :], wo[:, :], start=True, stop=True).then_inc(sem["brow_ps"], 1)

            def project(a, m):
                pe.wait_ge(*upto("oT_sb", a, m + 1))
                if m:
                    pe.wait_ge(*upto("res_sb", a, 2 * m))
                for t in range(2):
                    mm = nc.tensor.matmul(cols(PROJ, t), oT[:, m % 2, t * P:(t + 1) * P], wo[:, :], start=True, stop=True)
                mm.then_inc(sem["proj_ps"], 1)

            def attention(a):
                later = not is_first(a)
                pe.wait_ge(*upto("x_in", a, 16))
                if later:
                    pe.wait_ge(*upto("wT_sb", a - 1, 2))
                for h in range(NH):
                    for t in range(TPH):
                        mm = nc.tensor.transpose(cols(TURN[h], t), x_tok[:, TPH * h + t, :], ident[:, :])
                    mm.then_inc(sem["xT_ps"], 1)
                for h in range(NH):
                    pe.wait_ge(*upto(("xT_a", "xT_d")[h], a, 1))
                    nc.tensor.matmul(ps[:, SCORES[0] + h, :], wq_s[:, :], half(xT, h), start=True, stop=True).then_inc(sem["q_ps"], 1)
                    nc.tensor.matmul(ps[:, SCORES[1] + h, :], wk[:, :], half(xT, h), start=True, stop=True).then_inc(sem["k_ps"], 1)

                def values():
                    for h in range(NH):
                        for t in range(TPH):
                            mm = nc.tensor.matmul(cols(TURN[h], t), tile(xT, TPH * h + t), wv[:, :], start=True, stop=True)
                        mm.then_inc(sem["v_ps"], 1)

                def scores(j):
                    if j == 0:
                        for n in ("q_hi", "q_lo", "k_hi", "k_lo"):
                            pe.wait_ge(*upto(n, a, 2))
                    if j >= 2:
                        pe.wait_ge(*upto("probs_sb", a, j - 1))
                    for h in range(NH):
                        mm = split3(ps[:, SCORES[j % 2] + h, :], (tile(qT_hi, j), tile(qT_lo, j)), (half(kT_hi, h), half(kT_lo, h)))
                    mm.then_inc(sem["score_ps"], 1)

                def turn_probs(j):
                    pe.wait_ge(*upto("probs_sb", a, j + 1))
                    for h in range(NH):
                        if j == 0:
                            pe.wait_ge(*upto("v_lo_sb", a, h + 1))
                        else:
                            pe.wait_ge(*upto("pT_lo_sb", a, 2 * j - 1 + h))
                        for t in range(TPH):
                            mm = nc.tensor.transpose(cols(TURN[h], t), probs[:, j % 2, (TPH * h + t) * P:(TPH * h + t + 1) * P], ident[:, :])
                        mm.then_inc(sem["pT_ps"], 1)

                def mix(m, part):
                    if part == 0:
                        if m == 0 and later:
                            pe.wait_ge(*upto("y_sb", a - 1, 0))
                        if m:
                            pe.wait_ge(*upto("oT_sb", a, m))
                        pe.wait_ge(*upto("pT_lo_sb", a, 4 * (m + 1)))
                    for t in range(part * TPH, (part + 1) * TPH):
                        mm = split3(ps[:, PV, 0:2 * P], (v_hi[:, t, :], v_lo[:, t, :]),
                                    (pT_hi[:, m % 2, t, :], pT_lo[:, m % 2, t, :]), start=(t == 0), stop=(t == NT - 1))
                    if part == 1:
                        mm.then_inc(sem["pv_ps"], 1)

                scores(0)
                values()
                scores(1)
                for j in range(NT):
                    turn_probs(j)
                    if j + 2 < NT:
                        scores(j + 2)
                    if j >= 2:
                        mix(j // 2 - 1, j % 2)
                    if j >= 4 and j % 2 == 0:
                        project(a, j // 2 - 2)
                project(a, NT // 2 - 2)
                mix(NT // 2 - 1, 0)
                mix(NT // 2 - 1, 1)

            def turn_x1(a, h):
                pe.wait_ge(*upto("x1_sb", a, TPH * (h + 1)))
                for t in range(TPH):
                    mm = nc.tensor.transpose(cols(TURN[h], t), x1[:, TPH * h + t, :], ident[:, :])
                mm.then_inc(sem["x1T_ps"], 1)

            def logits(a):
                pe.wait_ge(*upto("x1T_sb", a, NH))
                pe.wait_ge(*upto("x1T_lo_sb", a, NH))
                for j in range(NT):
                    mm = nc.tensor.matmul(ps[:, TURN[0], j * E:(j + 1) * E], tile(x1T, j), gwT[:, :], start=True, stop=True)
                mm.then_inc(sem["logit_ps"], 1)

            def turn_weights(a, chunks):
                pe.wait_ge(*chunks)
                hold(pe)
                for h in range(NH):
                    for t in range(TPH):
                        mm = nc.tensor.transpose(ps[0:E, TURN[h], t * P:(t + 1) * P], w_tok[:, TPH * h + t, :], ident[:, :])
                    mm.then_inc(sem["wT_ps"], 1)

            def experts(b, ahead):
                xs = [(x1T_hi[:, b % 2, c * HALF:(c + 1) * HALF], x1T_lo[:, b % 2, c * HALF:(c + 1) * HALF]) for c in range(NH)]

                def gate_up(q, slot, c):
                    if c == 0:
                        pe.wait_ge(*upto("gu_hi_sb", b, q + 1))
                        pe.wait_ge(*upto("gu_lo_sb", b, q + 1))
                    if not is_first(q):
                        pe.wait_ge(*upto("silu_sb", b, NH * q + c - 1))
                        pe.wait_ge(*upto("m1_sb", b, NH * q + c - 1))
                    split3(ps[:, GATE[c], :], (gu_hi[:, slot, 0:P], gu_lo[:, slot, 0:P]), xs[c])
                    split3(ps[:, UP[c], :], (gu_hi[:, slot, P:2 * P], gu_lo[:, slot, P:2 * P]), xs[c]).then_inc(sem["gu_ps"], 1)

                def down(q, slot, c, stop=False):
                    if c == 0:
                        pe.wait_ge(*upto("dn_hi_sb", b, q + 1))
                        pe.wait_ge(*upto("dn_lo_sb", b, q + 1))
                    pe.wait_ge(*upto("hid_lo_sb", b, NH * q + c + 1))
                    split3(ps[:, SUM[c], :], (dn_hi[:, slot, :], dn_lo[:, slot, :]), (hid_hi[:, c, :], hid_lo[:, c, :]),
                           start=False, stop=stop).then_inc(sem["dn_ps"], 1)

                def pair(q, k):
                    for c in range(NH):
                        gate_up(q, (k + 1) % 2, c)
                    for c in range(NH):
                        down(q - 1, k % 2, c)

                pe.wait_ge(*upto("x1T_hi_sb", b, NH))
                pe.wait_ge(*upto("x1T_lo_sb", b, NH))
                gate_up(0, 0, 0)
                if ahead:
                    project(b + 1, NT // 2 - 1)
                gate_up(0, 0, 1)
                if ahead:
                    pe.wait_ge(*upto("res_sb", b + 1, NT))
                else:
                    pe.wait_ge(*upto("y_sb", b, 0))
                for c in range(NH):
                    nc.tensor.matmul(ps[:, SUM[c], :], identr[:, :], xs[c][0], start=True, stop=False)
                    nc.tensor.matmul(ps[:, SUM[c], :], identr[:, :], xs[c][1], start=False, stop=False)
                bodies = PAIRS // UNROLL
                if ahead:
                    for k in range(UNROLL):
                        pair(1 + k, k)
                        if k == 1:
                            turn_x1(b + 1, 0)
                            turn_x1(b + 1, 1)
                        if k == 2:
                            logits(b + 1)
                with pe.Fori(1 if ahead else 0, bodies) as i:
                    for k in range(UNROLL):
                        pair(UNROLL * i + 1 + k, k)
                for c in range(NH):
                    down(PAIRS, PAIRS % 2, c, stop=True)
                if ahead:
                    turn_weights(b + 1, upto("w_ready", b, NT // ROUTED_AT_ONCE))
                for c in range(NH):
                    pe.wait_ge(*upto("yT_sb", b, c + 1))
                    for t in range(TPH):
                        mm = nc.tensor.transpose(cols(SUM[c], t), yT[:, c, t * P:(t + 1) * P], ident[:, :])
                    mm.then_inc(sem["yt_ps"], 1)

            attention(0)
            project(0, NT // 2 - 1)
            turn_x1(0, 0)
            turn_x1(0, 1)
            logits(0)
            turn_weights(0, (sem["w_ready0"], 1))
            with pe.Fori(0, B - 1) as b:
                attention(b + 1)
                experts(b, ahead=True)
            experts(B - 1, ahead=False)

        @block.scalar
        def _(act):
            act.wait_ge(sem["const_in"], 16 * N_CONST)
            act.wait_ge(sem["const_dve"], 4)

            def copy(to, of):
                return nc.scalar.activation(to, of, ACT.Copy)

            def out_turned(a, m):
                act.wait_ge(*upto("pv_ps", a, m + 1))
                if m >= 2:
                    act.wait_ge(*upto("proj_ps", a, m - 1))
                copy(oT[:, m % 2, :], ps[:, PV, 0:2 * P]).then_inc(sem["oT_sb"], 1)

            def attention(a):
                act.wait_ge(*upto("xT_ps", a, 1))
                copy(half(xT, 0), ps[:, TURN[0], :]).then_inc(sem["xT_a"], 1)
                for h in range(NH):
                    act.wait_ge(*upto("q_ps", a, h + 1))
                    nc.scalar.activation(half(qT_hi, h), ps[:, SCORES[0] + h, :], ACT.Identity, bias=bq_s[:, 0:1]).then_inc(sem["q_hi"], 1)
                    act.wait_ge(*upto("k_ps", a, h + 1))
                    nc.scalar.activation(half(kT_hi, h), ps[:, SCORES[1] + h, :], ACT.Identity, bias=bias_cols[:, 1:2]).then_inc(sem["k_hi"], 1)

                def values_hi(h):
                    act.wait_ge(*upto("v_ps", a, h + 1))
                    copy(v_hi[:, TPH * h:TPH * (h + 1), :].rearrange("p t d -> p (t d)"), ps[:, TURN[h], :]).then_inc(sem["v_hi_sb"], 1)

                def exps(j):
                    act.wait_ge(*upto("max_sb", a, j + 1))
                    if j >= 2:
                        act.wait_ge(*upto("pT_ps", a, 2 * (j - 1)))
                    nc.scalar.activation(probs[:, j % 2, :], ps[:, SCORES[j % 2]:SCORES[j % 2] + 2, :].rearrange("p a b -> p (a b)"),
                                         ACT.Exp, bias=neg_max[:, j:j + 1], accum_out=row_sum[:, j:j + 1]).then_inc(sem["probs_sb"], 1)

                def probs_hi(j):
                    m = j // 2
                    if m >= 2 and j % 2 == 0:
                        act.wait_ge(*upto("pv_ps", a, m - 1))
                    for h in range(NH):
                        act.wait_ge(*upto("pT_ps", a, 2 * j + h + 1))
                        copy(pT_hi[:, m % 2, TPH * h:TPH * (h + 1), (j % 2) * P:(j % 2 + 1) * P],
                             ps[:, TURN[h], :].rearrange("p (t d) -> p t d", d=P)).then_inc(sem["pT_hi_sb"], 1)

                for h in range(NH):
                    values_hi(h)
                exps(0)
                for j in range(NT):
                    if j + 1 < NT:
                        exps(j + 1)
                    if j >= 4 and j % 2 == 0:
                        out_turned(a, j // 2 - 2)
                    probs_hi(j)
                out_turned(a, NT // 2 - 2)

            def turned_x1(a, h):
                act.wait_ge(*upto("x1T_ps", a, h + 1))
                copy(half(x1T, h), ps[:, TURN[h], :]).then_inc(sem["x1T_sb"], 1)
                copy(x1T_hi[:, a % 2, h * HALF:(h + 1) * HALF], ps[:, TURN[h], :]).then_inc(sem["x1T_hi_sb"], 1)

            def exp_logits(a):
                act.wait_ge(*upto("logit_ps", a, 1))
                nc.scalar.activation(exp_neg[:, :, :].rearrange("p t e -> p (t e)"), ps[:, TURN[0], :], ACT.Exp, scale=-1.0).then_inc(sem["exp_sb"], 1)

            def turned_weights(a):
                for h in range(NH):
                    act.wait_ge(*upto("wT_ps", a, h + 1))
                    copy(half(wT, h), ps[0:E, TURN[h], :]).then_inc(sem["wT_sb"], 1)

            def experts(b, ahead):
                def gu_split(q, raw, slot, loads):
                    act.wait_ge(sem[f"w_in{raw}"], b * PER[f"w_in{raw}"] + 16 * loads)
                    if not is_first_two(q):
                        act.wait_ge(*upto("gu_ps", b, NH * (q - 1)))
                    copy(gu_hi[:, slot, :], w_raw[:, raw, 0:2 * P]).then_inc(sem["gu_hi_sb"], 1)

                def dn_split(q, raw, slot):
                    if not is_first_two(q):
                        act.wait_ge(*upto("dn_ps", b, NH * (q - 1)))
                    copy(dn_hi[:, slot, :], w_raw[:, raw, 2 * P:3 * P]).then_inc(sem["dn_hi_sb"], 1)

                def silu(q, c):
                    act.wait_ge(*upto("gu_ps", b, NH * q + c + 1))
                    if not is_first(q):
                        act.wait_ge(*upto("m1_sb", b, NH * q + c - 1))
                    nc.scalar.activation(act_g[:, c, :], ps[:, GATE[c], :], ACT.Silu).then_inc(sem["silu_sb"], 1)

                def hid_split(q, c):
                    act.wait_ge(*upto("m2_sb", b, NH * q + c + 1))
                    if not is_first(q):
                        act.wait_ge(*upto("dn_ps", b, NH * q + c - 1))
                    copy(hid_hi[:, c, :], hid[:, c, :]).then_inc(sem["hid_hi_sb"], 1)

                def body(i, last=False, beside=False):
                    for k in range(UNROLL):
                        q = UNROLL * i + 1 + k
                        silu(q, 0)
                        if not (last and k == UNROLL - 1):
                            gu_split(q + 1, (k + 2) % UNROLL, k % 2, i + (1 if k + 2 < UNROLL else 2))
                        dn_split(q, (k + 1) % UNROLL, (k + 1) % 2)
                        silu(q, 1)
                        hid_split(q, 0)
                        hid_split(q, 1)
                        if beside and k == 1:
                            turned_x1(b + 1, 0)
                            turned_x1(b + 1, 1)
                        if beside and k == 2:
                            exp_logits(b + 1)

                act.wait_ge(*upto("y_sb", b, 0))
                gu_split(0, 0, 0, 1)
                dn_split(0, 0, 0)
                gu_split(1, 1, 1, 1)
                if ahead:
                    out_turned(b + 1, NT // 2 - 1)
                silu(0, 0)
                silu(0, 1)
                hid_split(0, 0)
                hid_split(0, 1)
                bodies = PAIRS // UNROLL
                if ahead:
                    body(0, beside=True)
                with act.Fori(1 if ahead else 0, bodies - 1) as i:
                    body(i)
                body(bodies - 1, last=True)
                for c in range(NH):
                    act.wait_ge(*upto("dn_ps", b, STEPS - 1 + c))
                    copy(yT[:, c, :], ps[:, SUM[c], :]).then_inc(sem["yT_sb"], 1)
                if ahead:
                    turned_weights(b + 1)

            attention(0)
            out_turned(0, NT // 2 - 1)
            for h in range(NH):
                turned_x1(0, h)
            exp_logits(0)
            turned_weights(0)
            with act.Fori(0, B - 1) as b:
                attention(b + 1)
                experts(b, ahead=True)
            experts(B - 1, ahead=False)

        @block.gpsimd
        def _(gp):
            gp.wait_ge(sem["brow_sb"], 1)

            def power(to, of):
                return nc.gpsimd.tensor_tensor(to, of, minus_half[:, :], ALU.pow)

            def subtract(to, a, hi):
                return nc.gpsimd.tensor_tensor(to, a, hi.bitcast(F32), ALU.subtract)

            def x_and_bias(a):
                gp.wait_ge(*upto("x_in", a, 16))
                nc.gpsimd.tensor_tensor(x_b[:, :, :], x_tok[:, :, :], b_row[:, :].unsqueeze(1).to_broadcast([P, NT, D]), ALU.add).then_inc(sem["xb_sb"], 1)

            def root(a, h):
                gp.wait_ge(*upto("ve_sb", a, h + 1))
                power(rstd[:, TPH * h:TPH * (h + 1)], var_eps[:, TPH * h:TPH * (h + 1)]).then_inc(sem["rstd_sb"], 1)

            def store_weights(a):
                gp.wait_ge(*upto("wT_sb", a, 2))
                hold(gp)
                gp.dma_start(w_scratch[a, :, :], wT[:, :]).then_inc(sem["wT_out"], 16)

            def experts(b, ahead):
                def gu_split(q, raw, slot):
                    gp.wait_ge(*upto("gu_hi_sb", b, q + 1))
                    subtract(gu_lo[:, slot, :], w_raw[:, raw, 0:2 * P], gu_hi[:, slot, :]).then_inc(sem["gu_lo_sb"], 1)

                def dn_split(q, raw, slot):
                    gp.wait_ge(*upto("dn_hi_sb", b, q + 1))
                    subtract(dn_lo[:, slot, :], w_raw[:, raw, 2 * P:3 * P], dn_hi[:, slot, :]).then_inc(sem["dn_lo_sb"], 1)

                def hid_split(q, c):
                    gp.wait_ge(*upto("hid_hi_sb", b, NH * q + c + 1))
                    subtract(hid_lo[:, c, :], hid[:, c, :], hid_hi[:, c, :]).then_inc(sem["hid_lo_sb"], 1)

                gu_split(0, 0, 0)
                dn_split(0, 0, 0)
                gu_split(1, 1, 1)
                hid_split(0, 0)
                hid_split(0, 1)
                if ahead:
                    root(b + 1, 1)

                def body(i, last=False):
                    for k in range(UNROLL):
                        q = UNROLL * i + 1 + k
                        if not (last and k == UNROLL - 1):
                            gu_split(q + 1, (k + 2) % UNROLL, k % 2)
                        dn_split(q, (k + 1) % UNROLL, (k + 1) % 2)
                        hid_split(q, 0)
                        hid_split(q, 1)

                with gp.Fori(0, PAIRS // UNROLL - 1) as i:
                    body(i)
                body(PAIRS // UNROLL - 1, last=True)
                if ahead:
                    store_weights(b + 1)
                for h in range(NH):
                    gp.wait_ge(*upto("ve2_sb", b, h + 1))
                    power(rstd2[:, TPH * h:TPH * (h + 1)], var_eps2[:, TPH * h:TPH * (h + 1)]).then_inc(sem["rstd2_sb"], 1)
                for h in range(NH):
                    gp.wait_ge(*upto("y_sb", b, TPH * (h + 1)))
                    hold(gp)
                    gp.dma_start(out[b, h * HALF:(h + 1) * HALF, :].rearrange("(t p) d -> p t d", p=P),
                                 y_out[:, TPH * h:TPH * (h + 1), :]).then_inc(sem["out_done"], 16)
                gp.wait_ge(*upto("out_done", b, 16 * NH))

            x_and_bias(0)
            root(0, 0)
            root(0, 1)
            store_weights(0)
            with gp.Fori(0, B - 1) as b:
                x_and_bias(b + 1)
                root(b + 1, 0)
                experts(b, ahead=True)
            experts(B - 1, ahead=False)

        @block.vector
        def _(ve):
            v = nc.vector
            v.memset(minus_half[:, :], -0.5).then_inc(sem["y_sb"], 1)
            ve.wait_ge(sem["const_in"], 16 * N_CONST)
            v.tensor_copy(bv_spread[:, :], bias_cols[:, 2:3].to_broadcast([P, P])).then_inc(sem["const_dve"], 1)
            v.tensor_copy(identr[:, :], ident[:, :]).then_inc(sem["const_dve"], 1)
            v.tensor_scalar(wq_s[:, :], wq[:, :], SCALE, None, ALU.mult).then_inc(sem["const_dve"], 1)
            v.tensor_scalar(bq_s[:, :], bias_cols[:, 0:1], SCALE, None, ALU.mult).then_inc(sem["const_dve"], 1)
            ve.wait_ge(sem["brow_ps"], 1)
            v.tensor_tensor(b_row[:, :], cols(PROJ, 0), bo_row[:, :], ALU.add).then_inc(sem["brow_sb"], 1)

            def rest(to, of, bias, hi):
                return v.scalar_tensor_tensor(out=to, in0=of, scalar=bias, in1=hi.bitcast(F32), op0=ALU.add, op1=ALU.subtract)

            def residual(a, m):
                two = slice(2 * m, 2 * m + 2)
                ve.wait_ge(*upto("probs_sb", a, 2 * m + 2))
                v.reciprocal(inv_sum[:, two], row_sum[:, two]).then_inc(sem["inv_sb"], 1)
                ve.wait_ge(*upto("inv_sb", a, m + 1))
                ve.wait_ge(*upto("proj_ps", a, m + 1))
                ve.wait_ge(*upto("xb_sb", a, 1))
                for j in (2 * m, 2 * m + 1):
                    v.scalar_tensor_tensor(out=x_res[:, j, :], in0=cols(PROJ, j % 2), scalar=inv_sum[:, j:j + 1],
                                           in1=x_b[:, j, :], op0=ALU.mult, op1=ALU.add).then_inc(sem["res_sb"], 1)

            def moments(a, h):
                quad = slice(TPH * h, TPH * (h + 1))
                for j in range(TPH * h, TPH * (h + 1)):
                    ve.wait_ge(*upto("res_sb", a, j + 1))
                    v.bn_stats(bn[:, j, :], x_res[:, j, :]).then_inc(sem["bn_sb"], 1)
                for j in range(TPH * h, TPH * (h + 1)):
                    ve.wait_ge(*upto("bn_sb", a, j + 1))
                    hold(ve)
                    v.bn_aggr(mv[:, j, :], bn[:, j, :]).then_inc(sem["mv_sb"], 1)
                ve.wait_ge(*upto("mv_sb", a, TPH * (h + 1)))
                v.tensor_scalar(var_eps[:, quad], mv[:, quad, 1], EPS, None, ALU.add).then_inc(sem["ve_sb"], 1)

            def normalise(a, h):
                ve.wait_ge(*upto("rstd_sb", a, h + 1))
                for j in range(TPH * h, TPH * (h + 1)):
                    v.tensor_scalar(x1[:, j, :], x_res[:, j, :], mv[:, j, 0:1], rstd[:, j:j + 1],
                                    ALU.subtract, ALU.mult).then_inc(sem["x1_sb"], 1)

            def attention(a):
                ve.wait_ge(*upto("xT_ps", a, 2))
                v.tensor_copy(half(xT, 1), ps[:, TURN[1], :]).then_inc(sem["xT_d"], 1)
                for h in range(NH):
                    ve.wait_ge(*upto("q_hi", a, h + 1))
                    rest(half(qT_lo, h), ps[:, SCORES[0] + h, :], bq_s[:, 0:1], half(qT_hi, h)).then_inc(sem["q_lo"], 1)
                    ve.wait_ge(*upto("k_hi", a, h + 1))
                    rest(half(kT_lo, h), ps[:, SCORES[1] + h, :], bias_cols[:, 1:2], half(kT_hi, h)).then_inc(sem["k_lo"], 1)

                def values_lo(h):
                    ve.wait_ge(*upto("v_hi_sb", a, h + 1))
                    v.tensor_tensor(v_lo[:, TPH * h:TPH * (h + 1), :].rearrange("p t d -> p (t d)"), ps[:, TURN[h], :],
                                    v_hi[:, TPH * h:TPH * (h + 1), :].rearrange("p t d -> p (t d)").bitcast(F32),
                                    ALU.subtract).then_inc(sem["v_lo_sb"], 1)

                def row_max(j):
                    ve.wait_ge(*upto("score_ps", a, j + 1))
                    v.tensor_reduce(neg_max[:, j:j + 1], ps[:, SCORES[j % 2]:SCORES[j % 2] + 2, :].rearrange("p a b -> p (a b)"),
                                    AX.X, ALU.max, negate=True).then_inc(sem["max_sb"], 1)

                def probs_lo(j):
                    m = j // 2
                    at = slice((j % 2) * P, (j % 2 + 1) * P)
                    for h in range(NH):
                        ve.wait_ge(*upto("pT_hi_sb", a, 2 * j + h + 1))
                        v.tensor_tensor(pT_lo[:, m % 2, TPH * h:TPH * (h + 1), at], ps[:, TURN[h], :].rearrange("p (t d) -> p t d", d=P),
                                        pT_hi[:, m % 2, TPH * h:TPH * (h + 1), at].bitcast(F32), ALU.subtract).then_inc(sem["pT_lo_sb"], 1)

                row_max(0)
                for h in range(NH):
                    values_lo(h)
                for j in range(NT):
                    if j + 1 < NT:
                        row_max(j + 1)
                    probs_lo(j)
                    if j >= 5 and j % 2 == 1:
                        residual(a, (j - 5) // 2)
                moments(a, 0)
                residual(a, 2)
                normalise(a, 0)

            def turned_x1_lo(a, h):
                ve.wait_ge(*upto("x1T_hi_sb", a, h + 1))
                v.tensor_tensor(x1T_lo[:, a % 2, h * HALF:(h + 1) * HALF], ps[:, TURN[h], :],
                                x1T_hi[:, a % 2, h * HALF:(h + 1) * HALF].bitcast(F32), ALU.subtract).then_inc(sem["x1T_lo_sb"], 1)

            class Chain:

                def __init__(self, name, start):
                    self.name, self.start, self.links = name, start, 0

                def before(self):
                    if self.links:
                        ve.wait_ge(sem[self.name], self.start + self.links)

                def link(self, instruction):
                    instruction.then_inc(sem[self.name], 1)
                    self.links += 1

            def sigmoid(a, chain):
                ve.wait_ge(*upto("exp_sb", a, 1))
                chain.link(v.tensor_scalar(denom[:, :, :], exp_neg[:, :, :], 1.0, None, ALU.add))
                chain.before()
                chain.link(v.reciprocal(sig[:, :, :], denom[:, :, :]))
                chain.before()
                chain.link(v.tensor_tensor(biased[:, :, :, :].rearrange("p t g e -> p t (g e)"), sig[:, :, :],
                                           gbias[:, :].unsqueeze(1).to_broadcast([P, NT, E]), ALU.add))

            def choose(part, chain, at, n, signal_name):
                def flat(m):
                    return m[:, 0:n, :, :].rearrange("p t g e -> p (t g) e")

                mine = biased[:, bass.ds(at, n), :, :].rearrange("p t g e -> p (t g) e")
                groups = [P, n, GROUPS, GROUPS]
                members = [P, n * GROUPS, PER_GROUP]
                other = g_score[:, 0:n, :].unsqueeze(2).to_broadcast(groups)
                own = g_score[:, 0:n, :].unsqueeze(3).to_broadcast(groups)
                experts_ = masked[:, 0:n, :, :].rearrange("p t g e -> p t (g e)")
                step = chain.link
                chain.before()
                if part == 0:
                    step(v.tensor_tensor(flat(hi4), mine[:, :, 0:4], mine[:, :, 4:8], ALU.max))
                    step(v.tensor_tensor(flat(lo4), mine[:, :, 0:4], mine[:, :, 4:8], ALU.min))
                elif part in (1, 3):
                    hi_a, hi_b, mn, w = ((hi4, hi2, mn2, 2), (hi2, hi1, mn1, 1))[part == 3]
                    step(v.tensor_tensor(flat(hi_b), flat(hi_a)[:, :, 0:w], flat(hi_a)[:, :, w:2 * w], ALU.max))
                    step(v.tensor_tensor(flat(mn), flat(hi_a)[:, :, 0:w], flat(hi_a)[:, :, w:2 * w], ALU.min))
                elif part in (2, 4):
                    lo_a, lo_b, mn, mx, w = ((lo4, lo2, mn2, mx2, 2), (lo2, lo1, mn1, mx1, 1))[part == 4]
                    step(v.tensor_tensor(flat(mx), flat(lo_a)[:, :, 0:w], flat(lo_a)[:, :, w:2 * w], ALU.max))
                    chain.before()
                    step(v.tensor_tensor(flat(lo_b), flat(mn), flat(mx), ALU.max))
                elif part == 5:
                    step(v.tensor_tensor(g_score[:, 0:n, :], hi1[:, 0:n, :, 0], lo1[:, 0:n, :, 0], ALU.add))
                    chain.before()
                    step(v.tensor_tensor(beats[:, 0:n, :, :], other, own, ALU.is_gt))
                elif part == 6:
                    step(v.tensor_tensor(ties[:, 0:n, :, :], other, own, ALU.is_equal))
                    chain.before()
                    step(v.tensor_tensor(ties[:, 0:n, :, :], ties[:, 0:n, :, :], lower[:, :, :].unsqueeze(1).to_broadcast(groups), ALU.mult))
                elif part == 7:
                    step(v.tensor_tensor(beaten[:, 0:n, :, :], beats[:, 0:n, :, :], ties[:, 0:n, :, :], ALU.add))
                    chain.before()
                    step(v.tensor_reduce(rank[:, 0:n, :], beaten[:, 0:n, :, :], AX.X, ALU.add))
                elif part == 8:
                    step(v.tensor_scalar(g_in[:, 0:n, :], rank[:, 0:n, :], TOP_GROUPS - 0.5, None, ALU.is_lt))
                    chain.before()
                    step(v.tensor_scalar(g_out[:, 0:n, :], g_in[:, 0:n, :], FAR, -FAR, ALU.mult, ALU.add))
                elif part == 9:
                    step(v.tensor_tensor(flat(kept), mine, g_in[:, 0:n, :].rearrange("p t g -> p (t g)").unsqueeze(2).to_broadcast(members), ALU.mult))
                    chain.before()
                    step(v.tensor_tensor(flat(masked), flat(kept), g_out[:, 0:n, :].rearrange("p t g -> p (t g)").unsqueeze(2).to_broadcast(members), ALU.add))
                elif part == 10:
                    hold(ve)
                    for t in range(n):
                        step(v.max(top8[:, t, :], experts_[:, t, :]))
                elif part == 11:
                    hold(ve)
                    for t in range(n):
                        step(v.match_replace(out=replaced[:, t, :], in_to_replace=top8[:, t, :], in_values=experts_[:, t, :], imm_value=GONE))
                elif part == 12:
                    step(v.tensor_tensor(chosen[:, 0:n, :], replaced[:, 0:n, :], experts_, ALU.not_equal))
                    chain.before()
                    step(v.tensor_tensor(w_raw8[:, 0:n, :], sig[:, bass.ds(at, n), :], chosen[:, 0:n, :], ALU.mult))
                elif part == 13:
                    step(v.tensor_reduce(w_sum[:, 0:n], w_raw8[:, 0:n, :], AX.X, ALU.add))
                    chain.before()
                    step(v.tensor_scalar(w_den[:, 0:n], w_sum[:, 0:n], 1e-20, None, ALU.add))
                elif part == 14:
                    step(v.reciprocal(w_inv[:, 0:n], w_den[:, 0:n]))
                    chain.before()
                    step(v.tensor_scalar(w_sum[:, 0:n], w_inv[:, 0:n], ROUTE_SCALE, None, ALU.mult))
                elif part == 15:
                    v.tensor_tensor(w_tok[:, bass.ds(at, n), :], w_raw8[:, 0:n, :], w_sum[:, 0:n].unsqueeze(2).to_broadcast([P, n, E]),
                                    ALU.mult).then_inc(sem[signal_name], 1)

            PARTS = 16

            def experts(b, ahead):
                def hidden(q, c, spread=None, loads=None, beside=None):
                    n = NH * q + c
                    ve.wait_ge(*upto("silu_sb", b, n + 1))
                    if not is_first(q):
                        ve.wait_ge(*upto("m2_sb", b, n - 1))
                    v.tensor_tensor(gated[:, c, :], act_g[:, c, :], ps[:, UP[c], :], ALU.mult).then_inc(sem["m1_sb"], 1)
                    if beside:
                        beside(0)
                    ve.wait_ge(*upto("m1_sb", b, n + 1))
                    if not is_first(q):
                        ve.wait_ge(*upto("hid_lo_sb", b, n - 1))
                        ve.wait_ge(sem[f"spread_in{spread}"], b * PER[f"spread_in{spread}"] + 32 * loads)
                        m2 = v.tensor_tensor(hid[:, c, :], gated[:, c, :], half(w_spread[:, spread, :], c), ALU.mult)
                    else:
                        m2 = v.tensor_copy(hid[:, c, :], gated[:, c, :])
                    m2.then_inc(sem["m2_sb"], 1)
                    if beside:
                        beside(1)

                def pair(i, k, beside=None):
                    for c in range(NH):
                        hidden(UNROLL * i + 1 + k, c, (k + 1) % UNROLL, i + 1,
                               beside and (lambda n: beside(4 * k + 2 * c + n)))

                bodies = PAIRS // UNROLL
                hidden(0, 0)
                if ahead:
                    residual(b + 1, NT // 2 - 1)
                hidden(0, 1)
                if ahead:
                    moments(b + 1, 1)
                    pair(0, 0)
                    normalise(b + 1, 1)
                    pair(0, 1)
                    turned_x1_lo(b + 1, 0)
                    turned_x1_lo(b + 1, 1)
                    pair(0, 2)
                    pair(0, 3)
                    sigmoid(b + 1, Chain("sigmoid", b * SIGMOID))
                    routed = 1 + NT // ROUTED_AT_ONCE
                    with ve.Fori(1, routed) as i:
                        chain = Chain("choose", (b * (NT // ROUTED_AT_ONCE) + i - 1) * CHOOSE)
                        ve.wait_ge(sem["sigmoid"], b * SIGMOID + SIGMOID)
                        for k in range(UNROLL):
                            pair(i, k, lambda n: choose(n, chain, (i - 1) * ROUTED_AT_ONCE, ROUTED_AT_ONCE, "w_ready"))
                        assert chain.links == CHOOSE
                    rest_of = routed
                else:
                    rest_of = 0
                with ve.Fori(rest_of, bodies) as i:
                    for k in range(UNROLL):
                        pair(i, k)

                for h in range(NH):
                    quad = slice(TPH * h, TPH * (h + 1))
                    ve.wait_ge(*upto("yt_ps", b, h + 1))
                    for t in range(TPH):
                        v.bn_stats(bn2[:, TPH * h + t, :], cols(SUM[h], t)).then_inc(sem["bn2_sb"], 1)
                    for t in range(TPH):
                        j = TPH * h + t
                        ve.wait_ge(*upto("bn2_sb", b, j + 1))
                        hold(ve)
                        v.bn_aggr(mv2[:, j, :], bn2[:, j, :]).then_inc(sem["mv2_sb"], 1)
                    ve.wait_ge(*upto("mv2_sb", b, TPH * (h + 1)))
                    v.tensor_scalar(var_eps2[:, quad], mv2[:, quad, 1], EPS, None, ALU.add).then_inc(sem["ve2_sb"], 1)
                for h in range(NH):
                    ve.wait_ge(*upto("rstd2_sb", b, h + 1))
                    for t in range(TPH):
                        j = TPH * h + t
                        v.tensor_scalar(y_out[:, j, :], cols(SUM[h], t), mv2[:, j, 0:1], rstd2[:, j:j + 1],
                                        ALU.subtract, ALU.mult).then_inc(sem["y_sb"], 1)

            attention(0)
            residual(0, NT // 2 - 1)
            moments(0, 1)
            normalise(0, 1)
            for h in range(NH):
                turned_x1_lo(0, h)
            chain = Chain("route0", 0)
            sigmoid(0, chain)
            for part in range(PARTS):
                choose(part, chain, 0, NT, "w_ready0")
            with ve.Fori(0, B - 1) as b:
                attention(b + 1)
                experts(b, ahead=True)
            experts(B - 1, ahead=False)


def is_first(n):
    return isinstance(n, int) and n == 0


def is_first_two(q):
    return isinstance(q, int) and q < 2


def kernel(**inputs):
    import numpy as np
    import concourse.bacc as bacc
    from concourse.bass_utils import run_bass_kernel_spmd

    a = {k: np.asarray(v) for k, v in inputs.items()}
    x = np.ascontiguousarray(a["L0_attn_x"])
    B, S, D = x.shape
    E, _, F = a["L0_ffn_We_gate"].shape

    def pairs(routed, shared, axis):
        all_ = np.concatenate([shared[None], np.zeros_like(shared)[None], routed])
        return np.concatenate([all_[0::2], all_[1::2]], axis=axis)

    w_pairs = np.concatenate([
        pairs(a["L0_ffn_We_gate"], a["L0_ffn_Ws_gate"], 2),
        pairs(a["L0_ffn_We_up"], a["L0_ffn_Ws_up"], 2),
        pairs(a["L0_ffn_We_down"], a["L0_ffn_Ws_down"], 1),
    ], axis=2)
    arrays = {
        "x": x,
        "w_qkvo": np.stack([a[f"L0_attn_W{i}"] for i in (1, 2, 3, 4)]),
        "b_qkvo": np.stack([a[f"L0_attn_b{i}"] for i in (1, 2, 3, 4)]),
        "gate_wT": np.ascontiguousarray(a["L0_ffn_gate_w"].T),
        "gate_bias": a["L0_ffn_gate_bias"][None],
        "w_pairs": np.ascontiguousarray(w_pairs),
        "ident_in": np.eye(P, dtype=np.float32),
        "lower_in": np.tril(np.ones((8, 8), np.float32), -1).reshape(1, -1),
    }
    nc = bacc.Bacc("TRN2", target_bir_lowering=False, num_devices=1)
    args = [nc.dram_tensor(n, v.shape, mybir.dt.from_np(v.dtype), kind="ExternalInput").ap() for n, v in arrays.items()]
    args.append(nc.dram_tensor("w_scratch", (B, E, S), F32, kind="Internal").ap())
    args.append(nc.dram_tensor("out", x.shape, F32, kind="ExternalOutput").ap())
    block_kernel(nc, *args)
    r = run_bass_kernel_spmd(nc, [arrays], core_ids=[0])
    return r.results[0]["out"]
```

```python
from contextlib import ExitStack

import concourse.bass as bass
from concourse import mybir

F32 = mybir.dt.float32
F32R = mybir.dt.float32r
ALU = mybir.AluOpType
ACT = mybir.ActivationFunctionType
AX = mybir.AxisListType

P = 128
HALF = 512
EPS = 1e-5
ROUTE_SCALE = 2.5
TOP_GROUPS = 4
FAR = 1e30
GONE = -3e38
UNROLL = 4


def block_kernel(nc, x, w_qkvo, b_qkvo, gate_wT, gate_bias, w_pairs, w_shared, ident_in, w_scratch, out):
    B, S, D = x.shape
    E = gate_wT.shape[1]
    F = P // 2
    GROUPS = 8
    PER_GROUP = E // GROUPS
    NT = S // P
    NH = S // HALF
    TPH = HALF // P
    PAIRS = E // 2
    QP = PAIRS + 1
    STEPS = QP * NH
    SCALE = float(D) ** -0.5
    assert D == P and NH == 2 and E == 64 and w_pairs.shape[0] == PAIRS and PAIRS % UNROLL == 0

    ctx = ExitStack()
    with ctx:
        def sb(name, shape, dt=F32):
            return ctx.enter_context(nc.sbuf_tensor(name, shape, dt))

        ident = sb("ident", [P, P])
        identr = sb("identr", [P, P], F32R)
        w_att = sb("w_att", [P, 4, P])
        wq, wk, wv, wo = (w_att[:, i, :] for i in range(4))
        wq_s = sb("wq_s", [P, P])
        bq_s = sb("bq_s", [P, 1])
        bias_cols = sb("bias_cols", [P, 4])
        bo_row = sb("bo_row", [P, P])
        bv_spread = sb("bv_spread", [P, P])
        b_row = sb("b_row", [P, P])
        gwT = sb("gwT", [P, E])
        gbias = sb("gbias", [P, E])
        minus_half = sb("minus_half", [P, TPH])
        x_tok = sb("x_tok", [P, NT, D])
        xT = sb("xT", [P, S])
        qT_hi, qT_lo, kT_hi, kT_lo = (sb(n, [P, S], F32R) for n in ("qT_hi", "qT_lo", "kT_hi", "kT_lo"))
        v_hi = sb("v_hi", [P, NT, D], F32R)
        v_lo = sb("v_lo", [P, NT, D], F32R)
        unread = sb("unread", [P, 1])
        neg_max = sb("neg_max", [P, NT])
        row_sum = sb("row_sum", [P, NT])
        inv_sum = sb("inv_sum", [P, NT])
        probs = sb("probs", [P, 2, S])
        pT_hi = sb("pT_hi", [P, 2, NT, 2 * P], F32R)
        pT_lo = sb("pT_lo", [P, 2, NT, 2 * P], F32R)
        pT_full = sb("pT_full", [P, NH, TPH, P])
        oT = sb("oT", [P, 2, 2 * P])
        x_b = sb("x_b", [P, NT, D])
        x_res = sb("x_res", [P, NT, D])
        x1 = sb("x1", [P, NT, D])
        bn = sb("bn", [P, NT, 6])
        mv = sb("mv", [P, NT, 2])
        var_eps = sb("var_eps", [P, NT])
        rstd = sb("rstd", [P, NT])
        x1T = sb("x1T", [P, S])
        x1T_hi = sb("x1T_hi", [P, 2, S], F32R)
        x1T_lo = sb("x1T_lo", [P, 2, S], F32R)
        exp_neg = sb("exp_neg", [P, NT, E])
        sig = sb("sig", [P, NT, E])
        biased = sb("biased", [P, NT, GROUPS, PER_GROUP])
        hi4, lo4 = (sb(n, [P, NT, GROUPS, 4]) for n in ("hi4", "lo4"))
        hi2, lo2, mn2, mx2 = (sb(n, [P, NT, GROUPS, 2]) for n in ("hi2", "lo2", "mn2", "mx2"))
        hi1, lo1, mn1, mx1 = (sb(n, [P, NT, GROUPS, 1]) for n in ("hi1", "lo1", "mn1", "mx1"))
        g_score = sb("g_score", [P, NT, GROUPS])
        g_top = sb("g_top", [P, NT, 8])
        picked = sb("picked", [P, NT, 8])
        g_left, g_in, g_cap = (sb(n, [P, NT, GROUPS]) for n in ("g_left", "g_in", "g_cap"))
        masked = sb("masked", [P, NT, GROUPS, PER_GROUP])
        top8 = sb("top8", [P, NT, 8])
        replaced, chosen, w_raw8 = (sb(n, [P, NT, E]) for n in ("replaced", "chosen", "w_raw8"))
        w_sum, w_den, w_inv, w_scale = (sb(n, [P, NT]) for n in ("w_sum", "w_den", "w_inv", "w_scale"))
        w_tok = sb("w_tok", [P, NT, E])
        wT = sb("wT", [E, S])
        w_raw = sb("w_raw", [P, UNROLL, 3 * P])
        shared_hi = sb("shared_hi", [P, 2 * P], F32R)
        shared_lo = sb("shared_lo", [P, 2 * P], F32R)
        gu_hi = sb("gu_hi", [P, UNROLL, 2 * P], F32R)
        gu_lo = sb("gu_lo", [P, UNROLL, 2 * P], F32R)
        dn_hi = sb("dn_hi", [P, 2, P], F32R)
        dn_lo = sb("dn_lo", [P, 2, P], F32R)
        w_spread = sb("w_spread", [P, UNROLL, S])
        act_g = sb("act_g", [P, 2, HALF])
        gated = sb("gated", [P, 2, HALF])
        hid = sb("hid", [P, 2, HALF])
        hid_hi = sb("hid_hi", [P, 2, HALF], F32R)
        hid_lo = sb("hid_lo", [P, 2, HALF], F32R)
        yT = sb("yT", [P, NH, HALF])
        bn2 = sb("bn2", [P, NT, 6])
        mv2 = sb("mv2", [P, NT, 2])
        var_eps2 = sb("var_eps2", [P, NT])
        rstd2 = sb("rstd2", [P, NT])
        y_out = sb("y_out", [P, NT, D])

        ps = ctx.enter_context(nc.psum_tensor("ps", [P, 8, HALF], F32))
        SCORES = (0, 2)
        TURN = (4, 5)
        PV, PROJ = 6, 7
        VALUES = (TURN, (PV, PROJ))
        GATE, UP, SUM = (0, 1), (2, 3), (6, 7)

        PER, FIRST, sem = {}, {}, {}

        def signal(name, per, first=0):
            PER[name], FIRST[name] = per, first
            sem[name] = ctx.enter_context(nc.semaphore(name))

        for name in ("ident_in", "w_att_in", "const_in", "shared_in", "hid_zero", "shared_hi_sb", "shared_lo_sb", "const_dve", "brow_ps", "brow_sb"):
            signal(name, 0)
        for h in range(NH):
            signal(f"x_in{h}", 16)
        for name, per in dict(
            exp_loaded=1, xT_ps=2, xT_a=1, xT_d=1, q_ps=2, k_ps=2, v_ps=2, q_hi=2, k_hi=2, v_hi_sb=2, q_lo=2, k_lo=2, v_lo_sb=2, xb_sb=1,
            score_ps=NT, max_sb=NT, probs_sb=NT, pT_ps=2 * NT, pT_hi_sb=2 * NT, pT_lo_sb=2 * NT,
            pv_ps=NT // 2, oT_sb=NT // 2, proj_ps=NT // 2, inv_sb=NT // 2, res_sb=NT, bn_sb=NT, mv_sb=NT, ve_sb=NH, rstd_sb=NH, x1_sb=NT,
            x1T_ps=2, x1T_sb=2, x1T_hi_sb=2, x1T_lo_sb=2, logit_ps=1, exp_sb=1, w_ready=1, wT_ps=2, wT_sb=2,
            gu_hi_sb=PAIRS, gu_lo_sb=PAIRS, dn_hi_sb=PAIRS, dn_lo_sb=PAIRS, gu_ps=STEPS, silu_sb=STEPS, m1_sb=STEPS, m2_sb=STEPS,
            hid_hi_a=QP, hid_hi_d=QP, hid_lo_sb=STEPS, dn_ps=STEPS,
            yT_sb=NH, yt_ps=NH, bn2_sb=NT, mv2_sb=NT, ve2_sb=NH, rstd2_sb=NH,
        ).items():
            signal(name, per)
        signal("y_sb", NT, first=1)
        signal("held", 0)
        signal("pT_full_sb", 0)
        signal("wT_out", 16)
        for k in range(UNROLL):
            signal(f"w_in{k}", 16 * (PAIRS // UNROLL))
            signal(f"spread_in{k}", 32 * (PAIRS // UNROLL))
        signal("out_done", 16 * NH)

        def upto(name, b, k):
            return sem[name], b * PER[name] + k + FIRST[name]

        def sum_bank(b, c):
            return (TURN if isinstance(b, int) and b == B - 1 else SUM)[c]

        def very_first(b, q, pairs=1):
            return is_first(b) and isinstance(q, int) and q < pairs

        def units(q):
            return slice(F, P) if is_first(q) else slice(0, P)

        def cols(bank, t):
            return ps[:, bank, t * P:(t + 1) * P]

        def tile(m, t):
            return m[:, t * P:(t + 1) * P]

        def half(m, h):
            return m[:, h * HALF:(h + 1) * HALF]

        def split3(to, lhs, rhs, start=True, stop=True):
            nc.tensor.matmul(to, lhs[0], rhs[0], start=start, stop=False)
            nc.tensor.matmul(to, lhs[0], rhs[1], start=False, stop=False)
            return nc.tensor.matmul(to, lhs[1], rhs[0], start=False, stop=stop)

        def hold(engine):
            engine.sem_inc(sem["held"], 1)

        PARTS, LINKS = 22, 27 + 4 * NT
        signal("routing", LINKS)

        block = ctx.enter_context(nc.Block())
        N_CONST = 4

        @block.sync
        def _(sp):
            def load_x(a):
                for h in range(NH):
                    sp.dma_start(x_tok[:, TPH * h:TPH * (h + 1), :], x[a, h * HALF:(h + 1) * HALF, :].rearrange("(t p) d -> p t d", p=P)).then_inc(sem[f"x_in{h}"], 16)

            load_x(0)
            sp.dma_start(bo_row[:, :], b_qkvo[3:4, :].to_broadcast([P, D])).then_inc(sem["const_in"], 16)
            sp.dma_start(gwT[:, :], gate_wT).then_inc(sem["const_in"], 16)
            sp.dma_start(gbias[:, :], gate_bias.to_broadcast([P, E])).then_inc(sem["const_in"], 16)

            sp.dma_start(w_raw[:, 0, 0:2 * P], w_shared).then_inc(sem["shared_in"], 16)

            def load_pair(q, slot):
                sp.dma_start(w_raw[:, slot, :], w_pairs[q - 1, :, :]).then_inc(sem[f"w_in{slot}"], 16)

            def load_spread(b, q, slot):
                for k in range(2):
                    row = w_scratch[b, 2 * q - 2 + k, :].rearrange("(o s) -> o s", o=1)
                    sp.dma_start(w_spread[k * F:(k + 1) * F, slot, :], row.to_broadcast([F, S])).then_inc(sem[f"spread_in{slot}"], 16)

            def slot_of(b, q):
                sp.wait_ge(*upto("dn_hi_sb", b, q - UNROLL))
                sp.wait_ge(*upto("gu_lo_sb", b, q - UNROLL))
                sp.wait_ge(*upto("dn_lo_sb", b, q - UNROLL))
                hold(sp)

            def store(b):
                for h in range(NH):
                    sp.wait_ge(*upto("y_sb", b, TPH * (h + 1)))
                    hold(sp)
                    sp.dma_start(out[b, h * HALF:(h + 1) * HALF, :].rearrange("(t p) d -> p t d", p=P),
                                 y_out[:, TPH * h:TPH * (h + 1), :]).then_inc(sem["out_done"], 16)
                sp.wait_ge(*upto("out_done", b, 16 * NH))
                hold(sp)

            def experts(b):
                for q in range(1, UNROLL + 1):
                    if not is_first(b):
                        slot_of(b, q)
                    elif q == UNROLL:
                        sp.wait_ge(sem["shared_hi_sb"], 1)
                        sp.wait_ge(sem["shared_lo_sb"], 1)
                    load_pair(q, q % UNROLL)
                sp.wait_ge(*upto("wT_out", b, 16))
                hold(sp)
                for q in range(1, UNROLL + 1):
                    if not is_first(b):
                        sp.wait_ge(*upto("m2_sb", b, NH * (q - UNROLL)))
                        hold(sp)
                    load_spread(b, q, q % UNROLL)

                def body(i):
                    for k in range(UNROLL):
                        q = UNROLL * i + 1 + k
                        slot_of(b, q)
                        load_pair(q, (k + 1) % UNROLL)
                        sp.wait_ge(*upto("m2_sb", b, NH * (q - UNROLL + 1)))
                        hold(sp)
                        load_spread(b, q, (k + 1) % UNROLL)

                body(1)
                if not is_first(b):
                    store(b - 1)
                with sp.Fori(2, PAIRS // UNROLL) as i:
                    body(i)

            def next_x(a):
                sp.wait_ge(*upto("xT_ps", a - 1, 2))
                hold(sp)
                sp.wait_ge(*upto("xb_sb", a - 1, 1))
                hold(sp)
                load_x(a)

            next_x(1)
            experts(0)
            with sp.Fori(1, B - 1) as b:
                next_x(b + 1)
                experts(b)
            experts(B - 1)
            store(B - 1)

        @block.tensor
        def _(pe):
            pe.wait_ge(sem["ident_in"], 16)

            def project(a, m):
                pe.wait_ge(*upto("oT_sb", a, m + 1))
                if m:
                    pe.wait_ge(*upto("res_sb", a, 2 * m))
                elif is_third_or_later(a):
                    pe.wait_ge(*upto("y_sb", a - 2, NT))
                for t in range(2):
                    mm = nc.tensor.matmul(cols(PROJ, t), oT[:, m % 2, t * P:(t + 1) * P], wo, start=True, stop=True)
                mm.then_inc(sem["proj_ps"], 1)

            def mix(a, m, part):
                if part == 0:
                    if m == 0 and is_third_or_later(a):
                        pe.wait_ge(*upto("y_sb", a - 2, TPH))
                    if m:
                        pe.wait_ge(*upto("oT_sb", a, m))
                    pe.wait_ge(*upto("pT_lo_sb", a, 4 * (m + 1)))
                for t in range(part * TPH, (part + 1) * TPH):
                    mm = split3(ps[:, PV, 0:2 * P], (v_hi[:, t, :], v_lo[:, t, :]),
                                (pT_hi[:, m % 2, t, :], pT_lo[:, m % 2, t, :]), start=(t == 0), stop=(t == NT - 1))
                if part == 1:
                    mm.then_inc(sem["pv_ps"], 1)

            def down(b, q, slot, c, stop=False):
                if is_first(q):
                    weights = (shared_hi[units(q), P:2 * P], shared_lo[units(q), P:2 * P])
                else:
                    weights = (dn_hi[:, slot, :], dn_lo[:, slot, :])
                    if c == 0:
                        pe.wait_ge(*upto("dn_hi_sb", b, q))
                        pe.wait_ge(*upto("dn_lo_sb", b, q))
                pe.wait_ge(*upto("hid_lo_sb", b, NH * q + c + 1))
                split3(ps[:, sum_bank(b, c), :], weights, (hid_hi[units(q), c, :], hid_lo[units(q), c, :]), start=False, stop=stop).then_inc(sem["dn_ps"], 1)

            def last_down(b, c):
                down(b, PAIRS, PAIRS % 2, c, stop=True)

            def turn_y(b, c):
                pe.wait_ge(*upto("yT_sb", b, c + 1))
                for t in range(TPH):
                    mm = nc.tensor.transpose(cols(sum_bank(b, c), t), yT[:, c, t * P:(t + 1) * P], ident[:, :])
                mm.then_inc(sem["yt_ps"], 1)

            def turn_weights(a):
                pe.wait_ge(*upto("w_ready", a, 1))
                hold(pe)
                for h in range(NH):
                    for t in range(TPH):
                        mm = nc.tensor.transpose(ps[0:E, TURN[h], t * P:(t + 1) * P], w_tok[:, TPH * h + t, :], ident[:, :])
                    mm.then_inc(sem["wT_ps"], 1)

            def turn_x1(a, h):
                pe.wait_ge(*upto("x1_sb", a, TPH * (h + 1)))
                for t in range(TPH):
                    mm = nc.tensor.transpose(cols(TURN[h], t), x1[:, TPH * h + t, :], ident[:, :])
                mm.then_inc(sem["x1T_ps"], 1)

            def logits(a):
                pe.wait_ge(*upto("x1T_sb", a, NH))
                pe.wait_ge(*upto("x1T_lo_sb", a, NH))
                for j in range(NT):
                    mm = nc.tensor.matmul(ps[:, TURN[0], j * E:(j + 1) * E], tile(x1T, j), gwT[:, :], start=True, stop=True)
                mm.then_inc(sem["logit_ps"], 1)

            def attention(a):
                if is_second(a):
                    pe.wait_ge(*upto("pT_lo_sb", 0, 2 * NT))
                elif not is_first(a):
                    pe.wait_ge(*upto("wT_sb", a - 1, 2))
                for h in range(NH):
                    pe.wait_ge(*upto(f"x_in{h}", a, 16))
                    for t in range(TPH):
                        mm = nc.tensor.transpose(cols(TURN[h], t), x_tok[:, TPH * h + t, :], ident[:, :])
                    mm.then_inc(sem["xT_ps"], 1)
                if is_first(a):
                    pe.wait_ge(sem["const_dve"], 5)
                if is_second(a):
                    project(0, NT // 2 - 2)
                    mix(0, NT // 2 - 1, 0)
                    mix(0, NT // 2 - 1, 1)
                for h in range(NH):
                    if is_third_or_later(a):
                        last_down(a - 2, h)
                    pe.wait_ge(*upto(("xT_a", "xT_d")[h], a, 1))
                    nc.tensor.matmul(ps[:, SCORES[0] + h, :], wq_s[:, :], half(xT, h), start=True, stop=True).then_inc(sem["q_ps"], 1)
                    nc.tensor.matmul(ps[:, SCORES[1] + h, :], wk, half(xT, h), start=True, stop=True).then_inc(sem["k_ps"], 1)
                    if is_second(a) and h == 0:
                        project(0, NT // 2 - 1)
                        turn_x1(0, 0)
                    if is_third_or_later(a) and h == 1:
                        turn_y(a - 2, 0)

                def values(h):
                    if is_first(a) and h == 0:
                        pe.wait_ge(sem["const_in"], 16 * N_CONST)
                    if is_second(a) and h == 0:
                        pe.wait_ge(*upto("res_sb", 0, NT))
                    for t in range(TPH):
                        mm = nc.tensor.matmul(cols(VALUES[is_second(a)][h], t), tile(xT, TPH * h + t), wv, start=True, stop=True)
                    mm.then_inc(sem["v_ps"], 1)

                def scores(j):
                    if j == 0:
                        for n in ("q_hi", "q_lo", "k_hi", "k_lo"):
                            pe.wait_ge(*upto(n, a, 2))
                    if j >= 2:
                        pe.wait_ge(*upto("probs_sb", a, j - 1))
                    for h in range(NH):
                        mm = split3(ps[:, SCORES[j % 2] + h, :], (tile(qT_hi, j), tile(qT_lo, j)), (half(kT_hi, h), half(kT_lo, h)))
                    mm.then_inc(sem["score_ps"], 1)

                def turn_probs(j):
                    pe.wait_ge(*upto("probs_sb", a, j + 1))
                    for h in range(NH):
                        if j == 0:
                            pe.wait_ge(*upto("v_lo_sb", a, h + 1))
                        elif is_second(a):
                            pe.wait_ge(sem["pT_full_sb"], 2 * j - 1 + h)
                        else:
                            pe.wait_ge(*upto("pT_lo_sb", a, 2 * j - 1 + h))
                        for t in range(TPH):
                            mm = nc.tensor.transpose(cols(TURN[h], t), probs[:, j % 2, (TPH * h + t) * P:(TPH * h + t + 1) * P], ident[:, :])
                        mm.then_inc(sem["pT_ps"], 1)

                values(0)
                if is_third_or_later(a):
                    turn_y(a - 2, 1)
                scores(0)
                values(1)
                if is_second(a):
                    turn_x1(0, 1)
                scores(1)
                if is_second(a):
                    logits(0)
                if is_first(a):
                    nc.tensor.matmul(cols(PROJ, 0), bv_spread[:, :], wo, start=True, stop=True).then_inc(sem["brow_ps"], 1)
                for j in range(NT):
                    if j + 2 < NT:
                        scores(j + 2)
                    if is_second(a) and j == 0:
                        pe.wait_ge(*upto("exp_sb", 0, 1))
                    turn_probs(j)
                    if j >= 2:
                        mix(a, j // 2 - 1, j % 2)
                    if j >= 4 and j % 2 == 0:
                        project(a, j // 2 - 2)

            def experts(b, ahead):
                xs = [(x1T_hi[:, b % 2, c * HALF:(c + 1) * HALF], x1T_lo[:, b % 2, c * HALF:(c + 1) * HALF]) for c in range(NH)]

                def gate_up(q, slot, c):
                    if is_first(b) and is_first(q):
                        pe.wait_ge(sem["shared_hi_sb"], 1)
                        pe.wait_ge(sem["shared_lo_sb"], 1)
                    if not is_first(q) and c == 0:
                        pe.wait_ge(*upto("gu_hi_sb", b, q))
                        pe.wait_ge(*upto("gu_lo_sb", b, q))
                    if not very_first(b, q):
                        pe.wait_ge(*upto("silu_sb", b, NH * q + c - 1))
                        pe.wait_ge(*upto("m1_sb", b, NH * q + c - 1))
                    if is_first(q):
                        split3(ps[:, GATE[c], :], (shared_hi[:, 0:P], shared_lo[:, 0:P]), xs[c]).then_inc(sem["gu_ps"], 1)
                    else:
                        split3(ps[:, GATE[c], :], (gu_hi[:, slot, 0:P], gu_lo[:, slot, 0:P]), xs[c])
                        split3(ps[:, UP[c], :], (gu_hi[:, slot, P:2 * P], gu_lo[:, slot, P:2 * P]), xs[c]).then_inc(sem["gu_ps"], 1)

                def seed():
                    if ahead:
                        pe.wait_ge(*upto("res_sb", b + 1, NT))
                    else:
                        pe.wait_ge(*upto("wT_sb", b, 2))
                    for c in range(NH):
                        nc.tensor.matmul(ps[:, sum_bank(b, c), :], identr[:, :], xs[c][0], start=True, stop=False)
                        nc.tensor.matmul(ps[:, sum_bank(b, c), :], identr[:, :], xs[c][1], start=False, stop=False)

                def turn_y_before():
                    turn_y(b - 1, 1)

                def pair(q, k, between=None):
                    for c in range(NH):
                        gate_up(q, (k + 1) % UNROLL, c)
                    if between:
                        between()
                    for c in range(NH):
                        down(b, q - 1, k % 2, c)

                pe.wait_ge(*upto("x1T_hi_sb", b, NH))
                pe.wait_ge(*upto("x1T_lo_sb", b, NH))
                if ahead:
                    gate_up(0, 0, 0)
                    if is_first(b):
                        pe.wait_ge(sem["pT_full_sb"], 2 * NT)
                        turn_weights(0)
                    project(b + 1, NT // 2 - 2)
                    mix(b + 1, NT // 2 - 1, 0)
                    mix(b + 1, NT // 2 - 1, 1)
                    gate_up(0, 0, 1)
                    project(b + 1, NT // 2 - 1)
                else:
                    gate_up(0, 0, 0)
                    seed()
                    last_down(b - 1, 0)
                    gate_up(0, 0, 1)
                    last_down(b - 1, 1)
                    turn_y(b - 1, 0)
                bodies = PAIRS // UNROLL
                for k in range(UNROLL):
                    pair(1 + k, k, between=(seed if ahead else turn_y_before) if k == 0 else None)
                    if ahead and k == 1:
                        turn_x1(b + 1, 0)
                        turn_x1(b + 1, 1)
                    if ahead and k == 2:
                        logits(b + 1)
                with pe.Fori(1, bodies - 1) as i:
                    for k in range(UNROLL):
                        pair(UNROLL * i + 1 + k, k)
                for k in range(UNROLL):
                    pair(UNROLL * (bodies - 1) + 1 + k, k)
                    if ahead and k == 0:
                        pe.wait_ge(*upto("exp_sb", b + 1, 1))
                        turn_weights(b + 1)

            attention(0)
            attention(1)
            experts(0, ahead=True)
            with pe.Fori(1, B - 1) as b:
                attention(b + 1)
                experts(b, ahead=True)
            experts(B - 1, ahead=False)
            for c in range(NH):
                last_down(B - 1, c)
            for c in range(NH):
                turn_y(B - 1, c)

        @block.scalar
        def _(act):
            act.dma_start(ident[:, :], ident_in).then_inc(sem["ident_in"], 16)
            act.dma_start(w_att[:, 0:2, :], w_qkvo[0:2, :, :].rearrange("n a b -> a n b")).then_inc(sem["w_att_in"], 16)
            with nc.allow_non_contiguous_dma(reason="four short bias columns"):
                act.dma_start(bias_cols[:, :], b_qkvo.rearrange("n d -> d n")).then_inc(sem["w_att_in"], 16)
            act.dma_start(w_att[:, 2:4, :], w_qkvo[2:4, :, :].rearrange("n a b -> a n b")).then_inc(sem["const_in"], 16)

            def load_exp(a):
                if is_first(a):
                    act.wait_ge(sem["const_dve"], 1)
                else:
                    act.wait_ge(*upto("exp_loaded", a, 0))
                nc.scalar.activation(unread[:, :], picked[:, 0, 0:1], ACT.Exp).then_inc(sem["exp_loaded"], 1)

            def copy(to, of):
                return nc.scalar.activation(to, of, ACT.Copy)

            def out_turned(a, m):
                act.wait_ge(*upto("pv_ps", a, m + 1))
                if m >= 2:
                    act.wait_ge(*upto("proj_ps", a, m - 1))
                copy(oT[:, m % 2, :], ps[:, PV, 0:2 * P]).then_inc(sem["oT_sb"], 1)

            def attention(a, prepare=None):
                if is_first(a):
                    load_exp(a)
                act.wait_ge(*upto("xT_ps", a, 1))
                copy(half(xT, 0), ps[:, TURN[0], :]).then_inc(sem["xT_a"], 1)
                if is_second(a):
                    out_turned(0, NT // 2 - 1)
                if is_first(a):
                    act.wait_ge(sem["const_dve"], 5)
                for h in range(NH):
                    if is_third_or_later(a):
                        summed(a - 2, h)
                    act.wait_ge(*upto("q_ps", a, h + 1))
                    nc.scalar.activation(half(qT_hi, h), ps[:, SCORES[0] + h, :], ACT.Identity, bias=bq_s[:, 0:1]).then_inc(sem["q_hi"], 1)
                    act.wait_ge(*upto("k_ps", a, h + 1))
                    nc.scalar.activation(half(kT_hi, h), ps[:, SCORES[1] + h, :], ACT.Identity, bias=bias_cols[:, 1:2]).then_inc(sem["k_hi"], 1)
                    if is_second(a) and h == 0:
                        turned_x1(0, 0)

                def values_hi(h):
                    act.wait_ge(*upto("v_ps", a, h + 1))
                    copy(v_hi[:, TPH * h:TPH * (h + 1), :].rearrange("p t d -> p (t d)"), ps[:, VALUES[is_second(a)][h], :]).then_inc(sem["v_hi_sb"], 1)

                def exps(j):
                    act.wait_ge(*upto("max_sb", a, j + 1))
                    if j >= 2:
                        act.wait_ge(*upto("pT_ps", a, 2 * (j - 1)))
                    nc.scalar.activation(probs[:, j % 2, :], ps[:, SCORES[j % 2]:SCORES[j % 2] + 2, :].rearrange("p a b -> p (a b)"),
                                         ACT.Exp, bias=neg_max[:, j:j + 1], accum_out=row_sum[:, j:j + 1]).then_inc(sem["probs_sb"], 1)

                def probs_hi(j):
                    m = j // 2
                    if m >= 2 and j % 2 == 0:
                        act.wait_ge(*upto("pv_ps", a, m - 1))
                    for h in range(NH):
                        act.wait_ge(*upto("pT_ps", a, 2 * j + h + 1))
                        copy(pT_hi[:, m % 2, TPH * h:TPH * (h + 1), (j % 2) * P:(j % 2 + 1) * P],
                             ps[:, TURN[h], :].rearrange("p (t d) -> p t d", d=P)).then_inc(sem["pT_hi_sb"], 1)
                        if is_second(a):
                            if j:
                                act.wait_ge(*upto("pT_lo_sb", a, 2 * j - 1 + h))
                            copy(pT_full[:, h, :, :], ps[:, TURN[h], :].rearrange("p (t d) -> p t d", d=P)).then_inc(sem["pT_full_sb"], 1)

                if not is_first(a):
                    load_exp(a)
                for h in range(NH):
                    values_hi(h)
                if is_second(a):
                    turned_x1(0, 1)
                exps(0)
                if is_second(a):
                    exp_logits(0)
                for j in range(NT):
                    if j + 1 < NT:
                        exps(j + 1)
                    if j >= 4 and j % 2 == 0:
                        out_turned(a, j // 2 - 2)
                    probs_hi(j)
                    if j == 2 and prepare:
                        prepare()
                    if j == 2 and is_first(a):
                        act.wait_ge(sem["shared_in"], 16)
                        copy(shared_hi[:, :], w_raw[:, 0, 0:2 * P]).then_inc(sem["shared_hi_sb"], 1)
                out_turned(a, NT // 2 - 2)

            def turned_x1(a, h):
                act.wait_ge(*upto("x1T_ps", a, h + 1))
                copy(half(x1T, h), ps[:, TURN[h], :]).then_inc(sem["x1T_sb"], 1)
                copy(x1T_hi[:, a % 2, h * HALF:(h + 1) * HALF], ps[:, TURN[h], :]).then_inc(sem["x1T_hi_sb"], 1)

            def exp_logits(a):
                act.wait_ge(*upto("logit_ps", a, 1))
                nc.scalar.activation(exp_neg[:, :, :].rearrange("p t e -> p (t e)"), ps[:, TURN[0], :], ACT.Exp, scale=-1.0).then_inc(sem["exp_sb"], 1)

            def turned_weights(a):
                for h in range(NH):
                    act.wait_ge(*upto("wT_ps", a, h + 1))
                    copy(half(wT, h), ps[0:E, TURN[h], :]).then_inc(sem["wT_sb"], 1)

            def gu_split(b, q, slot, loads):
                act.wait_ge(sem[f"w_in{slot}"], b * PER[f"w_in{slot}"] + 16 * loads)
                if not very_first(b, q, pairs=3):
                    act.wait_ge(*upto("gu_ps", b, NH * (q - 2)))
                copy(gu_hi[:, slot, :], w_raw[:, slot, 0:2 * P]).then_inc(sem["gu_hi_sb"], 1)

            def dn_split(b, q, raw, slot):
                if not very_first(b, q, pairs=3):
                    act.wait_ge(*upto("dn_ps", b, NH * (q - 1)))
                copy(dn_hi[:, slot, :], w_raw[:, raw, 2 * P:3 * P]).then_inc(sem["dn_hi_sb"], 1)

            def prepare(b):
                gu_split(b, 1, 1, 1)
                gu_split(b, 2, 2, 1)

            def summed(b, c):
                act.wait_ge(*upto("dn_ps", b, STEPS - 1 + c))
                copy(yT[:, c, :], ps[:, sum_bank(b, c), :]).then_inc(sem["yT_sb"], 1)

            def experts(b, ahead):
                def silu(q, c):
                    act.wait_ge(*upto("gu_ps", b, NH * q + c + 1))
                    if not very_first(b, q):
                        act.wait_ge(*upto("m1_sb", b, NH * q + c - 1))
                    gate = slice(0, F) if is_first(q) else slice(0, P)
                    nc.scalar.activation(act_g[units(q), c, :], ps[gate, GATE[c], :], ACT.Silu).then_inc(sem["silu_sb"], 1)

                def hid_split(q):
                    act.wait_ge(*upto("m2_sb", b, NH * q + 1))
                    if not very_first(b, q):
                        act.wait_ge(*upto("dn_ps", b, NH * q - 1))
                    copy(hid_hi[units(q), 0, :], hid[units(q), 0, :]).then_inc(sem["hid_hi_a"], 1)

                def body(i, last=False, beside=False):
                    for k in range(UNROLL):
                        q = UNROLL * i + 1 + k
                        silu(q, 0)
                        if not (last and k >= UNROLL - 2):
                            gu_split(b, q + 2, (k + 3) % UNROLL, i + (1 if k + 2 < UNROLL else 2))
                        dn_split(b, q, (k + 1) % UNROLL, (k + 1) % 2)
                        silu(q, 1)
                        hid_split(q)
                        if ahead and last and k == 0:
                            turned_weights(b + 1)
                        if beside and k == 1:
                            turned_x1(b + 1, 0)
                            turned_x1(b + 1, 1)
                        if beside and k == 2:
                            exp_logits(b + 1)

                silu(0, 0)
                if ahead:
                    if is_first(b):
                        turned_weights(0)
                    out_turned(b + 1, NT // 2 - 1)
                else:
                    summed(b - 1, 0)
                silu(0, 1)
                if not ahead:
                    summed(b - 1, 1)
                hid_split(0)
                bodies = PAIRS // UNROLL
                if ahead:
                    body(0, beside=True)
                with act.Fori(1 if ahead else 0, bodies - 1) as i:
                    body(i)
                body(bodies - 1, last=True)
            attention(0)
            attention(1, prepare=lambda: prepare(0))
            experts(0, ahead=True)
            with act.Fori(1, B - 1) as b:
                attention(b + 1, prepare=lambda: prepare(b))
                experts(b, ahead=True)
            prepare(B - 1)
            experts(B - 1, ahead=False)
            for c in range(NH):
                summed(B - 1, c)

        @block.gpsimd
        def _(gp):
            gp.wait_ge(sem["brow_sb"], 1)

            def power(to, of):
                return nc.gpsimd.tensor_tensor(to, of, minus_half[:, :], ALU.pow)

            def subtract(to, a, hi):
                return nc.gpsimd.tensor_tensor(to, a, hi.bitcast(F32), ALU.subtract)

            def x_and_bias(a):
                for h in range(NH):
                    gp.wait_ge(*upto(f"x_in{h}", a, 16))
                nc.gpsimd.tensor_tensor(x_b[:, :, :], x_tok[:, :, :], b_row[:, :].unsqueeze(1).to_broadcast([P, NT, D]), ALU.add).then_inc(sem["xb_sb"], 1)

            def root(a, h):
                gp.wait_ge(*upto("ve_sb", a, h + 1))
                power(rstd[:, TPH * h:TPH * (h + 1)], var_eps[:, TPH * h:TPH * (h + 1)]).then_inc(sem["rstd_sb"], 1)

            def store_weights(a):
                gp.wait_ge(*upto("wT_sb", a, 2))
                hold(gp)
                gp.dma_start(w_scratch[a, :, :], wT[:, :]).then_inc(sem["wT_out"], 16)

            def root_y(b, h):
                gp.wait_ge(*upto("ve2_sb", b, h + 1))
                power(rstd2[:, TPH * h:TPH * (h + 1)], var_eps2[:, TPH * h:TPH * (h + 1)]).then_inc(sem["rstd2_sb"], 1)

            def gu_split(b, q, slot):
                gp.wait_ge(*upto("gu_hi_sb", b, q))
                subtract(gu_lo[:, slot, :], w_raw[:, slot, 0:2 * P], gu_hi[:, slot, :]).then_inc(sem["gu_lo_sb"], 1)

            def dn_split(b, q, raw, slot):
                gp.wait_ge(*upto("dn_hi_sb", b, q))
                subtract(dn_lo[:, slot, :], w_raw[:, raw, 2 * P:3 * P], dn_hi[:, slot, :]).then_inc(sem["dn_lo_sb"], 1)

            def prepare(b):
                for q in (1, 2):
                    gu_split(b, q, q)

            def experts(b, ahead):
                def hid_split(q, c):
                    gp.wait_ge(*upto(("hid_hi_a", "hid_hi_d")[c], b, q + 1))
                    subtract(hid_lo[:, c, :], hid[:, c, :], hid_hi[:, c, :]).then_inc(sem["hid_lo_sb"], 1)

                hid_split(0, 0)
                hid_split(0, 1)
                if ahead:
                    root(b + 1, 1)

                def body(i, last=False, finish=False):
                    for k in range(UNROLL):
                        q = UNROLL * i + 1 + k
                        if not (last and k >= UNROLL - 2):
                            gu_split(b, q + 2, (k + 3) % UNROLL)
                        dn_split(b, q, (k + 1) % UNROLL, (k + 1) % 2)
                        if finish and k == 0:
                            for h in range(NH):
                                root_y(b - 1, h)
                        hid_split(q, 0)
                        hid_split(q, 1)

                if not ahead:
                    body(0, finish=True)
                with gp.Fori(0 if ahead else 1, PAIRS // UNROLL - 1) as i:
                    body(i)
                body(PAIRS // UNROLL - 1, last=True)
                if ahead:
                    store_weights(b + 1)

            x_and_bias(0)
            gp.wait_ge(sem["shared_hi_sb"], 1)
            subtract(shared_lo[:, :], w_raw[:, 0, 0:2 * P], shared_hi[:, :]).then_inc(sem["shared_lo_sb"], 1)
            root(0, 0)
            root(0, 1)
            x_and_bias(1)
            for j in range(NT):
                at = slice((j % 2) * P, (j % 2 + 1) * P)
                for h in range(NH):
                    gp.wait_ge(sem["pT_full_sb"], 2 * j + h + 1)
                    quad = slice(TPH * h, TPH * (h + 1))
                    subtract(pT_lo[:, (j // 2) % 2, quad, at], pT_full[:, h, :, :], pT_hi[:, (j // 2) % 2, quad, at]).then_inc(sem["pT_lo_sb"], 1)
                if j == 3:
                    prepare(0)
            root(1, 0)
            store_weights(0)
            experts(0, ahead=True)
            with gp.Fori(1, B - 1) as b:
                for h in range(NH):
                    root_y(b - 1, h)
                x_and_bias(b + 1)
                prepare(b)
                root(b + 1, 0)
                experts(b, ahead=True)
            prepare(B - 1)
            experts(B - 1, ahead=False)
            for h in range(NH):
                root_y(B - 1, h)

        @block.vector
        def _(ve):
            v = nc.vector
            v.memset(minus_half[:, :], -0.5).then_inc(sem["y_sb"], 1)
            v.memset(picked[:, :, :], GONE).then_inc(sem["const_dve"], 1)
            ve.wait_ge(sem["ident_in"], 16)
            v.tensor_copy(identr[:, :], ident[:, :]).then_inc(sem["const_dve"], 1)
            ve.wait_ge(sem["w_att_in"], 32)
            v.tensor_scalar(wq_s[:, :], wq, SCALE, None, ALU.mult).then_inc(sem["const_dve"], 1)
            v.tensor_scalar(bq_s[:, :], bias_cols[:, 0:1], SCALE, None, ALU.mult).then_inc(sem["const_dve"], 1)
            v.tensor_copy(bv_spread[:, :], bias_cols[:, 2:3].to_broadcast([P, P])).then_inc(sem["const_dve"], 1)

            v.memset(hid[:, :, :], 0.0).then_inc(sem["hid_zero"], 1)
            ve.wait_ge(sem["hid_zero"], 1)
            v.tensor_copy(hid_hi[:, :, :], hid[:, :, :]).then_inc(sem["hid_zero"], 1)

            def rest(to, of, bias, hi):
                return v.scalar_tensor_tensor(out=to, in0=of, scalar=bias, in1=hi.bitcast(F32), op0=ALU.add, op1=ALU.subtract)

            def residual(a, m):
                two = slice(2 * m, 2 * m + 2)
                ve.wait_ge(*upto("probs_sb", a, 2 * m + 2))
                v.reciprocal(inv_sum[:, two], row_sum[:, two]).then_inc(sem["inv_sb"], 1)
                ve.wait_ge(*upto("inv_sb", a, m + 1))
                ve.wait_ge(*upto("proj_ps", a, m + 1))
                ve.wait_ge(*upto("xb_sb", a, 1))
                for j in (2 * m, 2 * m + 1):
                    v.scalar_tensor_tensor(out=x_res[:, j, :], in0=cols(PROJ, j % 2), scalar=inv_sum[:, j:j + 1],
                                           in1=x_b[:, j, :], op0=ALU.mult, op1=ALU.add).then_inc(sem["res_sb"], 1)

            def moments(a, h):
                quad = slice(TPH * h, TPH * (h + 1))
                for j in range(TPH * h, TPH * (h + 1)):
                    ve.wait_ge(*upto("res_sb", a, j + 1))
                    v.bn_stats(bn[:, j, :], x_res[:, j, :]).then_inc(sem["bn_sb"], 1)
                for j in range(TPH * h, TPH * (h + 1)):
                    ve.wait_ge(*upto("bn_sb", a, j + 1))
                    hold(ve)
                    v.bn_aggr(mv[:, j, :], bn[:, j, :]).then_inc(sem["mv_sb"], 1)
                ve.wait_ge(*upto("mv_sb", a, TPH * (h + 1)))
                v.tensor_scalar(var_eps[:, quad], mv[:, quad, 1], EPS, None, ALU.add).then_inc(sem["ve_sb"], 1)

            def normalise(a, h):
                ve.wait_ge(*upto("rstd_sb", a, h + 1))
                for j in range(TPH * h, TPH * (h + 1)):
                    v.tensor_scalar(x1[:, j, :], x_res[:, j, :], mv[:, j, 0:1], rstd[:, j:j + 1],
                                    ALU.subtract, ALU.mult).then_inc(sem["x1_sb"], 1)

            def moments_y(b, h):
                quad = slice(TPH * h, TPH * (h + 1))
                ve.wait_ge(*upto("yt_ps", b, h + 1))
                for t in range(TPH):
                    v.bn_stats(bn2[:, TPH * h + t, :], cols(sum_bank(b, h), t)).then_inc(sem["bn2_sb"], 1)
                for t in range(TPH):
                    j = TPH * h + t
                    ve.wait_ge(*upto("bn2_sb", b, j + 1))
                    hold(ve)
                    v.bn_aggr(mv2[:, j, :], bn2[:, j, :]).then_inc(sem["mv2_sb"], 1)
                ve.wait_ge(*upto("mv2_sb", b, TPH * (h + 1)))
                v.tensor_scalar(var_eps2[:, quad], mv2[:, quad, 1], EPS, None, ALU.add).then_inc(sem["ve2_sb"], 1)

            def normalise_y(b, h):
                ve.wait_ge(*upto("rstd2_sb", b, h + 1))
                for t in range(TPH):
                    j = TPH * h + t
                    v.tensor_scalar(y_out[:, j, :], cols(sum_bank(b, h), t), mv2[:, j, 0:1], rstd2[:, j:j + 1],
                                    ALU.subtract, ALU.mult).then_inc(sem["y_sb"], 1)

            def attention(a):
                ve.wait_ge(*upto("xT_ps", a, 2))
                v.tensor_copy(half(xT, 1), ps[:, TURN[1], :]).then_inc(sem["xT_d"], 1)
                if is_second(a):
                    residual(0, NT // 2 - 2)
                    normalise(0, 0)
                for h in range(NH):
                    ve.wait_ge(*upto("q_hi", a, h + 1))
                    rest(half(qT_lo, h), ps[:, SCORES[0] + h, :], bq_s[:, 0:1], half(qT_hi, h)).then_inc(sem["q_lo"], 1)
                    ve.wait_ge(*upto("k_hi", a, h + 1))
                    rest(half(kT_lo, h), ps[:, SCORES[1] + h, :], bias_cols[:, 1:2], half(kT_hi, h)).then_inc(sem["k_lo"], 1)
                    if is_second(a) and h == 0:
                        residual(0, NT // 2 - 1)
                    if is_second(a) and h == 1:
                        moments(0, 1)
                    if is_third_or_later(a) and h == 1:
                        moments_y(a - 2, 0)
                def values_lo(h):
                    ve.wait_ge(*upto("v_hi_sb", a, h + 1))
                    v.tensor_tensor(v_lo[:, TPH * h:TPH * (h + 1), :].rearrange("p t d -> p (t d)"), ps[:, VALUES[is_second(a)][h], :],
                                    v_hi[:, TPH * h:TPH * (h + 1), :].rearrange("p t d -> p (t d)").bitcast(F32),
                                    ALU.subtract).then_inc(sem["v_lo_sb"], 1)

                def row_max(j):
                    ve.wait_ge(*upto("score_ps", a, j + 1))
                    v.tensor_reduce(neg_max[:, j:j + 1], ps[:, SCORES[j % 2]:SCORES[j % 2] + 2, :].rearrange("p a b -> p (a b)"),
                                    AX.X, ALU.max, negate=True).then_inc(sem["max_sb"], 1)

                def probs_lo(j):
                    m = j // 2
                    at = slice((j % 2) * P, (j % 2 + 1) * P)
                    for h in range(NH):
                        ve.wait_ge(*upto("pT_hi_sb", a, 2 * j + h + 1))
                        v.tensor_tensor(pT_lo[:, m % 2, TPH * h:TPH * (h + 1), at], ps[:, TURN[h], :].rearrange("p (t d) -> p t d", d=P),
                                        pT_hi[:, m % 2, TPH * h:TPH * (h + 1), at].bitcast(F32), ALU.subtract).then_inc(sem["pT_lo_sb"], 1)

                values_lo(0)
                if is_second(a):
                    normalise(0, 1)
                row_max(0)
                values_lo(1)
                if is_second(a):
                    turned_x1_lo(0, 0)
                    turned_x1_lo(0, 1)
                row_max(1)
                if is_first(a):
                    ve.wait_ge(sem["const_in"], 16 * N_CONST)
                    ve.wait_ge(sem["brow_ps"], 1)
                    v.tensor_tensor(b_row[:, :], cols(PROJ, 0), bo_row[:, :], ALU.add).then_inc(sem["brow_sb"], 1)
                if is_second(a):
                    routing = Chain(0)
                for j in range(NT):
                    if j + 2 < NT:
                        row_max(j + 2)
                    if not is_second(a):
                        probs_lo(j)
                    if is_third_or_later(a) and j == 2:
                        moments_y(a - 2, 1)
                    if is_third_or_later(a) and j in (1, 3):
                        normalise_y(a - 2, j // 2)
                    if is_second(a):
                        for part in range(PARTS * j // (NT - 1), PARTS * (j + 1) // (NT - 1)) if j < NT - 1 else ():
                            choose(0, part, routing)
                    if j >= 5 and j % 2 == 1:
                        residual(a, (j - 5) // 2)
                moments(a, 0)

            def turned_x1_lo(a, h):
                ve.wait_ge(*upto("x1T_hi_sb", a, h + 1))
                v.tensor_tensor(x1T_lo[:, a % 2, h * HALF:(h + 1) * HALF], ps[:, TURN[h], :],
                                x1T_hi[:, a % 2, h * HALF:(h + 1) * HALF].bitcast(F32), ALU.subtract).then_inc(sem["x1T_lo_sb"], 1)

            class Chain:

                def __init__(self, start):
                    self.start, self.links = start, 0

                def before(self):
                    ve.wait_ge(sem["routing"], self.start + self.links)

                def link(self, instruction):
                    instruction.then_inc(sem["routing"], 1)
                    self.links += 1

            def choose(a, part, chain):
                def flat(m):
                    return m[:, :, :, :].rearrange("p t g e -> p (t g) e")

                scored = masked[:, :, :, :].rearrange("p t g e -> p t (g e)")
                step = chain.link
                if part == 0:
                    ve.wait_ge(*upto("exp_sb", a, 1))
                else:
                    chain.before()
                if part == 0:
                    step(v.tensor_scalar(exp_neg[:, :, :], exp_neg[:, :, :], 1.0, None, ALU.add))
                elif part < 5:
                    quarter = slice((part - 1) * NT // 4, part * NT // 4)
                    step(v.reciprocal(sig[:, quarter, :], exp_neg[:, quarter, :]))
                elif part == 5:
                    step(v.tensor_tensor(biased[:, :, :, :].rearrange("p t g e -> p t (g e)"), sig[:, :, :],
                                         gbias[:, :].unsqueeze(1).to_broadcast([P, NT, E]), ALU.add))
                elif part == 6:
                    step(v.tensor_tensor(flat(hi4), flat(biased)[:, :, 0:4], flat(biased)[:, :, 4:8], ALU.max))
                    step(v.tensor_tensor(flat(lo4), flat(biased)[:, :, 0:4], flat(biased)[:, :, 4:8], ALU.min))
                elif part in (7, 8):
                    hi_a, lo_a, hi_b, lo_b, mn, mx, w = ((hi4, lo4, hi2, lo2, mn2, mx2, 2), (hi2, lo2, hi1, lo1, mn1, mx1, 1))[part - 7]
                    step(v.tensor_tensor(flat(mn), flat(hi_a)[:, :, 0:w], flat(hi_a)[:, :, w:2 * w], ALU.min))
                    step(v.tensor_tensor(flat(mx), flat(lo_a)[:, :, 0:w], flat(lo_a)[:, :, w:2 * w], ALU.max))
                    step(v.tensor_tensor(flat(hi_b), flat(hi_a)[:, :, 0:w], flat(hi_a)[:, :, w:2 * w], ALU.max))
                    chain.before()
                    step(v.tensor_tensor(flat(lo_b), flat(mn), flat(mx), ALU.max))
                elif part == 9:
                    step(v.tensor_tensor(g_score[:, :, :], hi1[:, :, :, 0], lo1[:, :, :, 0], ALU.add))
                    chain.before()
                    hold(ve)
                    for t in range(NT):
                        step(v.max(g_top[:, t, :], g_score[:, t, :]))
                elif part == 10:
                    step(v.tensor_copy(picked[:, :, 0:TOP_GROUPS], g_top[:, :, 0:TOP_GROUPS]))
                    chain.before()
                    hold(ve)
                    for t in range(NT):
                        step(v.match_replace(out=g_left[:, t, :], in_to_replace=picked[:, t, :], in_values=g_score[:, t, :], imm_value=GONE))
                elif part == 11:
                    step(v.tensor_tensor(g_in[:, :, :], g_left[:, :, :], g_score[:, :, :], ALU.not_equal))
                    chain.before()
                    step(v.tensor_scalar(g_cap[:, :, :], g_in[:, :, :], 2 * FAR, -FAR, ALU.mult, ALU.add))
                elif part == 12:
                    step(v.tensor_tensor(flat(masked), flat(biased), g_cap[:, :, :].rearrange("p t g -> p (t g)").unsqueeze(2).to_broadcast([P, NT * GROUPS, PER_GROUP]), ALU.min))
                elif part in (13, 14):
                    hold(ve)
                    for t in range((part - 13) * TPH, (part - 12) * TPH):
                        step(v.max(top8[:, t, :], scored[:, t, :]))
                elif part in (15, 16):
                    hold(ve)
                    for t in range((part - 15) * TPH, (part - 14) * TPH):
                        step(v.match_replace(out=replaced[:, t, :], in_to_replace=top8[:, t, :], in_values=scored[:, t, :], imm_value=GONE))
                elif part == 17:
                    step(v.tensor_tensor(chosen[:, :, :], replaced[:, :, :], scored, ALU.not_equal))
                elif part == 18:
                    step(v.tensor_tensor(w_raw8[:, :, :], sig[:, :, :], chosen[:, :, :], ALU.mult))
                elif part == 19:
                    step(v.tensor_reduce(w_sum[:, :], w_raw8[:, :, :], AX.X, ALU.add))
                elif part == 20:
                    step(v.tensor_scalar(w_den[:, :], w_sum[:, :], 1e-20, None, ALU.add))
                    chain.before()
                    step(v.reciprocal(w_inv[:, :], w_den[:, :]))
                    chain.before()
                    step(v.tensor_scalar(w_scale[:, :], w_inv[:, :], ROUTE_SCALE, None, ALU.mult))
                elif part == 21:
                    v.tensor_tensor(w_tok[:, :, :], w_raw8[:, :, :], w_scale[:, :].unsqueeze(2).to_broadcast([P, NT, E]),
                                    ALU.mult).then_inc(sem["w_ready"], 1)

            def experts(b, ahead):
                def hidden(q, c, spread=None, loads=None):
                    n = NH * q + c
                    ve.wait_ge(*upto("silu_sb", b, n + 1))
                    if not very_first(b, q):
                        ve.wait_ge(*upto("m2_sb", b, n - 1))
                    up = GATE[c] if is_first(q) else UP[c]
                    v.tensor_tensor(gated[units(q), c, :], act_g[units(q), c, :], ps[units(q), up, :], ALU.mult).then_inc(sem["m1_sb"], 1)
                    ve.wait_ge(*upto("m1_sb", b, n + 1))
                    if not very_first(b, q):
                        ve.wait_ge(*upto("hid_lo_sb", b, n - 1))
                    if not is_first(q):
                        ve.wait_ge(sem[f"spread_in{spread}"], b * PER[f"spread_in{spread}"] + 32 * loads)
                        m2 = v.tensor_tensor(hid[:, c, :], gated[:, c, :], half(w_spread[:, spread, :], c), ALU.mult)
                    else:
                        m2 = v.tensor_copy(hid[units(q), c, :], gated[units(q), c, :])
                    m2.then_inc(sem["m2_sb"], 1)
                    if c == 1:
                        ve.wait_ge(*upto("m2_sb", b, n + 1))
                        if not very_first(b, q):
                            ve.wait_ge(*upto("dn_ps", b, n - 1))
                        v.tensor_copy(hid_hi[units(q), 1, :], hid[units(q), 1, :]).then_inc(sem["hid_hi_d"], 1)

                def pair(i, k):
                    for c in range(NH):
                        hidden(UNROLL * i + 1 + k, c, (k + 1) % UNROLL, i + 1)

                bodies = PAIRS // UNROLL
                if ahead:
                    residual(b + 1, NT // 2 - 2)
                hidden(0, 0)
                if ahead:
                    normalise(b + 1, 0)
                    residual(b + 1, NT // 2 - 1)
                else:
                    moments_y(b - 1, 0)
                hidden(0, 1)
                if not ahead:
                    moments_y(b - 1, 1)
                if ahead:
                    moments(b + 1, 1)
                    pair(0, 0)
                    normalise(b + 1, 1)
                    pair(0, 1)
                    turned_x1_lo(b + 1, 0)
                    turned_x1_lo(b + 1, 1)
                    pair(0, 2)
                    pair(0, 3)
                    routing = Chain((b + 1) * LINKS)
                    rest_of = 1 - (-PARTS // UNROLL)
                    for n in range(UNROLL * (rest_of - 1)):
                        pair(1 + n // UNROLL, n % UNROLL)
                        if n < PARTS:
                            choose(b + 1, n, routing)
                    assert routing.links == LINKS
                else:
                    for k in range(UNROLL):
                        pair(0, k)
                        if k < NH:
                            normalise_y(b - 1, k)
                    rest_of = 1
                with ve.Fori(rest_of, bodies) as i:
                    for k in range(UNROLL):
                        pair(i, k)

            attention(0)
            attention(1)
            experts(0, ahead=True)
            with ve.Fori(1, B - 1) as b:
                attention(b + 1)
                experts(b, ahead=True)
            experts(B - 1, ahead=False)
            for h in range(NH):
                moments_y(B - 1, h)
            for h in range(NH):
                normalise_y(B - 1, h)


def is_first(n):
    return isinstance(n, int) and n == 0


def is_second(n):
    return isinstance(n, int) and n == 1


def is_third_or_later(n):
    return not (isinstance(n, int) and n < 2)


def kernel(**inputs):
    import numpy as np
    import concourse.bacc as bacc
    from concourse.bass_utils import run_bass_kernel_spmd

    a = {k: np.asarray(v) for k, v in inputs.items()}
    x = np.ascontiguousarray(a["L0_attn_x"])
    B, S, D = x.shape
    E, _, F = a["L0_ffn_We_gate"].shape

    def side_by_side(w, axis):
        return np.concatenate([w[0::2], w[1::2]], axis=axis)

    w_pairs = np.concatenate([side_by_side(a[f"L0_ffn_We_{n}"], axis) for n, axis in (("gate", 2), ("up", 2), ("down", 1))], axis=2)
    w_shared = np.zeros((P, 2 * P), np.float32)
    w_shared[:, 0:F] = a["L0_ffn_Ws_gate"]
    w_shared[:, F:P] = a["L0_ffn_Ws_up"]
    w_shared[F:P, P:2 * P] = a["L0_ffn_Ws_down"]
    arrays = {
        "x": x,
        "w_qkvo": np.stack([a[f"L0_attn_W{i}"] for i in (1, 2, 3, 4)]),
        "b_qkvo": np.stack([a[f"L0_attn_b{i}"] for i in (1, 2, 3, 4)]),
        "gate_wT": np.ascontiguousarray(a["L0_ffn_gate_w"].T),
        "gate_bias": a["L0_ffn_gate_bias"][None],
        "w_pairs": np.ascontiguousarray(w_pairs),
        "w_shared": w_shared,
        "ident_in": np.eye(P, dtype=np.float32),
    }
    nc = bacc.Bacc("TRN2", target_bir_lowering=False, num_devices=1)
    args = [nc.dram_tensor(n, v.shape, mybir.dt.from_np(v.dtype), kind="ExternalInput").ap() for n, v in arrays.items()]
    args.append(nc.dram_tensor("w_scratch", (B, E, S), F32, kind="Internal").ap())
    args.append(nc.dram_tensor("out", x.shape, F32, kind="ExternalOutput").ap())
    block_kernel(nc, *args)
    r = run_bass_kernel_spmd(nc, [arrays], core_ids=[0])
    return r.results[0]["out"]
```
